# Optimizing a Trainium2 kernel written in Bass

```python
import numpy as np
import jax
import jax.numpy as jnp

def _softmax(x, axis=-1):
    return jax.nn.softmax(x, axis=axis)
def _gelu(x):
    return jax.nn.gelu(x, approximate=True)
def _silu(x):
    return jax.nn.silu(x)
def _sigmoid(x):
    return jax.nn.sigmoid(x)
def _layernorm(x, axis=-1, eps=1e-5):
    m = jnp.mean(x, axis=axis, keepdims=True)
    v = jnp.var(x, axis=axis, keepdims=True)
    return (x - m) / jnp.sqrt(v + eps)
def _scatter_add(tgt, idx, src, axis=0):
    return tgt.at[idx].add(src)
def _segment_sum(src, seg, n):
    return jax.ops.segment_sum(src, seg, n)

kernel_name = 'mk_conv_preact_d2_conv_nhwc256_313a43'

def setup_inputs(seed: int = 0):
    np.random.seed(seed)
    _w = jnp.asarray
    def _rec_inputs():
        import jax
        import jax.numpy as jnp
        _gk = jax.random.key(seed)
        x = -0.0003929 + 0.9999 * jax.random.normal(jax.random.fold_in(_gk, 1), (4, 128, 128, 256), jnp.float32)
        return x
    x = _rec_inputs()
    def _L0_conv_setup():
        import jax, jax.numpy as jnp
        import numpy as np
        from jax import lax

        def layer_norm(x, g, b, eps=1e-05):
            mu = jnp.mean(x, axis=-1, keepdims=True)
            var = jnp.var(x, axis=-1, keepdims=True)
            return (x - mu) / jnp.sqrt(var + eps) * g + b

        def selective_scan(u, delta, A, Bm, Cm, D):
            Bsz, L, d_inner = u.shape
            N = A.shape[1]

            def step(h, inp):
                u_t, d_t, B_t, C_t = inp
                dA = jnp.exp(d_t[..., None] * A)
                h = dA * h + (d_t * u_t)[..., None] * B_t[:, None, :]
                y = jnp.einsum('bdn,bn->bd', h, C_t)
                return (h, y)
            h0 = jnp.zeros((Bsz, d_inner, N), dtype=u.dtype)
            xs = (u.transpose(1, 0, 2), delta.transpose(1, 0, 2), Bm.transpose(1, 0, 2), Cm.transpose(1, 0, 2))
            _, ys = lax.scan(step, h0, xs)
            return ys.transpose(1, 0, 2) + u * D

        def mamba_block(x, in_proj_w, conv_w, conv_b, x_proj_w, dt_proj_w, dt_proj_b, A_log, D, out_proj_w):
            d_inner = in_proj_w.shape[0] // 2
            d_state = A_log.shape[1]
            dt_rank = dt_proj_w.shape[1]
            d_conv = conv_w.shape[-1]
            xz = x @ in_proj_w.T
            xi, z = jnp.split(xz, 2, axis=-1)
            xt = xi.transpose(0, 2, 1)
            kernel = conv_w[:, None, :]
            xc = lax.conv_general_dilated(xt, kernel, (1,), [(d_conv - 1, 0)], feature_group_count=d_inner, dimension_numbers=('NCH', 'OIH', 'NCH'))
            xc = xc + conv_b[None, :, None]
            xs = jax.nn.silu(xc).transpose(0, 2, 1)
            x_dbl = xs @ x_proj_w.T
            dt, Bm, Cm = jnp.split(x_dbl, [dt_rank, dt_rank + d_state], axis=-1)
            delta = jax.nn.softplus(dt @ dt_proj_w.T + dt_proj_b)
            A = -jnp.exp(A_log)
            y = selective_scan(xs, delta, A, Bm, Cm, D)
            y = y * jax.nn.silu(z)
            return y @ out_proj_w.T
        key = jax.random.key(seed)
        ks = jax.random.split(key, 12)
        B, H, W, C = (4, 128, 128, 256)
        d_state, d_conv, expand = (16, 4, 2)
        d_inner = expand * C
        dt_rank = int(np.ceil(C / 16))
        s = 0.02
        A = jnp.tile(jnp.arange(1, d_state + 1, dtype=jnp.float32)[None, :], (d_inner, 1))
        dt0 = jax.random.uniform(ks[9], (d_inner,), minval=0.001, maxval=0.1)
        return {'x': jax.random.normal(ks[0], (B, H, W, C), jnp.float32), 'ln_g': jnp.ones((C,), jnp.float32), 'ln_b': jnp.zeros((C,), jnp.float32), 'in_proj_w': jax.random.normal(ks[1], (2 * d_inner, C), jnp.float32) * s, 'conv_w': jax.random.normal(ks[2], (d_inner, d_conv), jnp.float32) * s, 'conv_b': jnp.zeros((d_inner,), jnp.float32), 'x_proj_w': jax.random.normal(ks[3], (dt_rank + 2 * d_state, d_inner), jnp.float32) * s, 'dt_proj_w': jax.random.normal(ks[4], (d_inner, dt_rank), jnp.float32) * dt_rank ** (-0.5), 'dt_proj_b': jnp.log(jnp.expm1(dt0)), 'A_log': jnp.log(A), 'D': jnp.ones((d_inner,), jnp.float32), 'out_proj_w': jax.random.normal(ks[5], (C, d_inner), jnp.float32) * s, 'proj_w': jax.random.normal(ks[6], (C, C), jnp.float32) * s, 'proj_b': jnp.zeros((C,), jnp.float32), 'skip_scale': jnp.ones((1,), jnp.float32)}
    _L0_conv_all = _L0_conv_setup()
    _L0_conv_in = {k: v for k, v in _L0_conv_all.items() if k in ('ln_g', 'ln_b', 'in_proj_w', 'conv_w', 'conv_b', 'x_proj_w', 'dt_proj_w', 'dt_proj_b', 'A_log', 'D', 'out_proj_w', 'proj_w', 'proj_b', 'skip_scale', )}
    del _L0_conv_all

    def _L1_conv_setup():
        import jax, jax.numpy as jnp
        import numpy as np
        B, H, W, C = (8, 128, 128, 256)
        K, DT, EPS = (5, 0.2, 0.001)
        LAM2 = 4.0

        def _dwconv(x, w):
            k = w.reshape(3, 3, 1, C)
            return jax.lax.conv_general_dilated(x, k, (1, 1), 'SAME', dimension_numbers=('NHWC', 'HWIO', 'NHWC'), feature_group_count=C)

        def _bn(x, gamma, beta, mean, var):
            return (x - mean) * jax.lax.rsqrt(var + EPS) * gamma + beta

        def _sobel(x):
            xp = jnp.pad(x, ((0, 0), (1, 1), (1, 1), (0, 0)), mode='reflect')
            top, mid, bot = (xp[:, :-2], xp[:, 1:-1], xp[:, 2:])
            gy = bot[:, :, :-2] + 2 * bot[:, :, 1:-1] + bot[:, :, 2:] - (top[:, :, :-2] + 2 * top[:, :, 1:-1] + top[:, :, 2:])
            gx = top[:, :, 2:] + 2 * mid[:, :, 2:] + bot[:, :, 2:] - (top[:, :, :-2] + 2 * mid[:, :, :-2] + bot[:, :, :-2])
            return (gy, gx)
        key = jax.random.key(seed)
        ks = jax.random.split(key, 6)
        f = jnp.float32
        d = {}
        d['s0'] = jax.random.normal(ks[0], (B, H, W, C), f)
        d['wg'] = jax.random.normal(ks[1], (3, 3, C), f) * 0.1
        d['wg1'] = jax.random.normal(ks[2], (3, 3, C), f) * 0.1
        for i, p in enumerate(['g', 'g1', 'out']):
            k4 = jax.random.split(ks[3 + i], 4)
            d[p + '_gamma'] = 1.0 + 0.1 * jax.random.normal(k4[0], (C,), f)
            d[p + '_beta'] = 0.1 * jax.random.normal(k4[1], (C,), f)
            d[p + '_mean'] = 0.1 * jax.random.normal(k4[2], (C,), f)
            d[p + '_var'] = 0.5 + jax.random.uniform(k4[3], (C,), f)
        return d
    _L1_conv_all = _L1_conv_setup()
    _L1_conv_in = {k: v for k, v in _L1_conv_all.items() if k in ('wg', 'wg1', 'g_gamma', 'g_beta', 'g_mean', 'g_var', 'g1_gamma', 'g1_beta', 'g1_mean', 'g1_var', 'out_gamma', 'out_beta', 'out_mean', 'out_var', )}
    del _L1_conv_all

    return {
        "x": x,
        "L0_conv_ln_g": _L0_conv_in["ln_g"],
        "L0_conv_ln_b": _L0_conv_in["ln_b"],
        "L0_conv_in_proj_w": _L0_conv_in["in_proj_w"],
        "L0_conv_conv_w": _L0_conv_in["conv_w"],
        "L0_conv_conv_b": _L0_conv_in["conv_b"],
        "L0_conv_x_proj_w": _L0_conv_in["x_proj_w"],
        "L0_conv_dt_proj_w": _L0_conv_in["dt_proj_w"],
        "L0_conv_dt_proj_b": _L0_conv_in["dt_proj_b"],
        "L0_conv_A_log": _L0_conv_in["A_log"],
        "L0_conv_D": _L0_conv_in["D"],
        "L0_conv_out_proj_w": _L0_conv_in["out_proj_w"],
        "L0_conv_proj_w": _L0_conv_in["proj_w"],
        "L0_conv_proj_b": _L0_conv_in["proj_b"],
        "L0_conv_skip_scale": _L0_conv_in["skip_scale"],
        "L1_conv_wg": _L1_conv_in["wg"],
        "L1_conv_wg1": _L1_conv_in["wg1"],
        "L1_conv_g_gamma": _L1_conv_in["g_gamma"],
        "L1_conv_g_beta": _L1_conv_in["g_beta"],
        "L1_conv_g_mean": _L1_conv_in["g_mean"],
        "L1_conv_g_var": _L1_conv_in["g_var"],
        "L1_conv_g1_gamma": _L1_conv_in["g1_gamma"],
        "L1_conv_g1_beta": _L1_conv_in["g1_beta"],
        "L1_conv_g1_mean": _L1_conv_in["g1_mean"],
        "L1_conv_g1_var": _L1_conv_in["g1_var"],
        "L1_conv_out_gamma": _L1_conv_in["out_gamma"],
        "L1_conv_out_beta": _L1_conv_in["out_beta"],
        "L1_conv_out_mean": _L1_conv_in["out_mean"],
        "L1_conv_out_var": _L1_conv_in["out_var"],
    }

def reference(x, L0_conv_ln_g, L0_conv_ln_b, L0_conv_in_proj_w, L0_conv_conv_w, L0_conv_conv_b, L0_conv_x_proj_w, L0_conv_dt_proj_w, L0_conv_dt_proj_b, L0_conv_A_log, L0_conv_D, L0_conv_out_proj_w, L0_conv_proj_w, L0_conv_proj_b, L0_conv_skip_scale, L1_conv_wg, L1_conv_wg1, L1_conv_g_gamma, L1_conv_g_beta, L1_conv_g_mean, L1_conv_g_var, L1_conv_g1_gamma, L1_conv_g1_beta, L1_conv_g1_mean, L1_conv_g1_var, L1_conv_out_gamma, L1_conv_out_beta, L1_conv_out_mean, L1_conv_out_var):
    import jax
    import jax.numpy as jnp
    def _L0_conv_ref(x, ln_g, ln_b, in_proj_w, conv_w, conv_b, x_proj_w, dt_proj_w, dt_proj_b, A_log, D, out_proj_w, proj_w, proj_b, skip_scale):
        import jax, jax.numpy as jnp
        import numpy as np
        from jax import lax

        def layer_norm(x, g, b, eps=1e-05):
            mu = jnp.mean(x, axis=-1, keepdims=True)
            var = jnp.var(x, axis=-1, keepdims=True)
            return (x - mu) / jnp.sqrt(var + eps) * g + b

        def selective_scan(u, delta, A, Bm, Cm, D):
            Bsz, L, d_inner = u.shape
            N = A.shape[1]

            def step(h, inp):
                u_t, d_t, B_t, C_t = inp
                dA = jnp.exp(d_t[..., None] * A)
                h = dA * h + (d_t * u_t)[..., None] * B_t[:, None, :]
                y = jnp.einsum('bdn,bn->bd', h, C_t)
                return (h, y)
            h0 = jnp.zeros((Bsz, d_inner, N), dtype=u.dtype)
            xs = (u.transpose(1, 0, 2), delta.transpose(1, 0, 2), Bm.transpose(1, 0, 2), Cm.transpose(1, 0, 2))
            _, ys = lax.scan(step, h0, xs)
            return ys.transpose(1, 0, 2) + u * D

        def mamba_block(x, in_proj_w, conv_w, conv_b, x_proj_w, dt_proj_w, dt_proj_b, A_log, D, out_proj_w):
            d_inner = in_proj_w.shape[0] // 2
            d_state = A_log.shape[1]
            dt_rank = dt_proj_w.shape[1]
            d_conv = conv_w.shape[-1]
            xz = x @ in_proj_w.T
            xi, z = jnp.split(xz, 2, axis=-1)
            xt = xi.transpose(0, 2, 1)
            kernel = conv_w[:, None, :]
            xc = lax.conv_general_dilated(xt, kernel, (1,), [(d_conv - 1, 0)], feature_group_count=d_inner, dimension_numbers=('NCH', 'OIH', 'NCH'))
            xc = xc + conv_b[None, :, None]
            xs = jax.nn.silu(xc).transpose(0, 2, 1)
            x_dbl = xs @ x_proj_w.T
            dt, Bm, Cm = jnp.split(x_dbl, [dt_rank, dt_rank + d_state], axis=-1)
            delta = jax.nn.softplus(dt @ dt_proj_w.T + dt_proj_b)
            A = -jnp.exp(A_log)
            y = selective_scan(xs, delta, A, Bm, Cm, D)
            y = y * jax.nn.silu(z)
            return y @ out_proj_w.T
        B, H, W, C = x.shape
        xc = x.transpose(0, 3, 1, 2)
        L = H * W
        x_flat = xc.reshape(B, C, L).transpose(0, 2, 1)
        x_norm = layer_norm(x_flat, ln_g, ln_b)
        y = mamba_block(x_norm, in_proj_w, conv_w, conv_b, x_proj_w, dt_proj_w, dt_proj_b, A_log, D, out_proj_w)
        y = y + skip_scale * x_norm
        y = layer_norm(y, ln_g, ln_b)
        y = y @ proj_w.T + proj_b
        out = y.transpose(0, 2, 1).reshape(B, -1, H, W)
        return out.transpose(0, 2, 3, 1)

    def _L1_conv_ref(s0, wg, wg1, g_gamma, g_beta, g_mean, g_var, g1_gamma, g1_beta, g1_mean, g1_var, out_gamma, out_beta, out_mean, out_var):
        import jax, jax.numpy as jnp
        import numpy as np
        B, H, W, C = (8, 128, 128, 256)
        K, DT, EPS = (5, 0.2, 0.001)
        LAM2 = 4.0

        def _dwconv(x, w):
            k = w.reshape(3, 3, 1, C)
            return jax.lax.conv_general_dilated(x, k, (1, 1), 'SAME', dimension_numbers=('NHWC', 'HWIO', 'NHWC'), feature_group_count=C)

        def _bn(x, gamma, beta, mean, var):
            return (x - mean) * jax.lax.rsqrt(var + EPS) * gamma + beta

        def _sobel(x):
            xp = jnp.pad(x, ((0, 0), (1, 1), (1, 1), (0, 0)), mode='reflect')
            top, mid, bot = (xp[:, :-2], xp[:, 1:-1], xp[:, 2:])
            gy = bot[:, :, :-2] + 2 * bot[:, :, 1:-1] + bot[:, :, 2:] - (top[:, :, :-2] + 2 * top[:, :, 1:-1] + top[:, :, 2:])
            gx = top[:, :, 2:] + 2 * mid[:, :, 2:] + bot[:, :, 2:] - (top[:, :, :-2] + 2 * mid[:, :, :-2] + bot[:, :, :-2])
            return (gy, gx)
        fsrc = s0
        h = s0
        h0 = fsrc
        g = jax.nn.relu(_bn(_dwconv(h, wg), g_gamma, g_beta, g_mean, g_var))
        g1 = jax.nn.relu(_bn(_dwconv(h, wg1), g1_gamma, g1_beta, g1_mean, g1_var))
        gy, gx = _sobel(h)
        Dx = 1.0 / (gy * gy / LAM2 + 1.0)
        Dy = 1.0 / (gx * gx / LAM2 + 1.0)
        ux = 0.5 * (jnp.roll(g, 1, axis=2) - jnp.roll(g, -1, axis=2))
        vy = 0.5 * (jnp.roll(g1, 1, axis=3) - jnp.roll(g1, -1, axis=3))
        Ax, Ay = (g * DT, g1 * DT)
        Bx, By = (Dx * DT, Dy * DT)
        E = (ux + vy) * DT
        D = 1.0 / (1.0 + 2.0 * Bx + 2.0 * By)
        cm_x, cp_x = (-Ax + 2.0 * Bx, Ax + 2.0 * Bx)
        cm_y, cp_y = (-Ay + 2.0 * By, Ay + 2.0 * By)
        c0 = 1.0 - 2.0 * Bx - 2.0 * By
        for _ in range(K):
            prev = h
            h = D * (c0 * h0 - 2.0 * E * h + cm_x * jnp.roll(h, 1, axis=2) + cp_x * jnp.roll(h, -1, axis=2) + cm_y * jnp.roll(h, 1, axis=3) + cp_y * jnp.roll(h, -1, axis=3))
            h = h + D * (2.0 * DT) * fsrc
            h0 = prev
        return jax.nn.relu(_bn(h, out_gamma, out_beta, out_mean, out_var))

    def _gn(v, G=32, eps=1e-5):
        B_, H_, W_, C_ = v.shape
        g = v.reshape(B_, H_, W_, G, C_ // G)
        m = jnp.mean(g, axis=(1, 2, 4), keepdims=True)
        s = jnp.var(g, axis=(1, 2, 4), keepdims=True)
        return ((g - m) / jnp.sqrt(s + eps)).reshape(v.shape)

    def _ln_c(v, eps=1e-6):
        m = jnp.mean(v, axis=-1, keepdims=True)
        s = jnp.var(v, axis=-1, keepdims=True)
        return (v - m) / jnp.sqrt(s + eps)

    def _ln_t(v, eps=1e-5):
        m = jnp.mean(v, axis=-1, keepdims=True)
        s = jnp.var(v, axis=-1, keepdims=True)
        return (v - m) / jnp.sqrt(s + eps)

    def _to_tokens(v):
        B_, H_, W_, C_ = v.shape
        return v.reshape(B_, H_ * W_, C_)
    def _from_tokens(t, like):
        return t.reshape(like.shape)

    x = x + _L0_conv_ref(_gn(x), L0_conv_ln_g, L0_conv_ln_b, L0_conv_in_proj_w, L0_conv_conv_w, L0_conv_conv_b, L0_conv_x_proj_w, L0_conv_dt_proj_w, L0_conv_dt_proj_b, L0_conv_A_log, L0_conv_D, L0_conv_out_proj_w, L0_conv_proj_w, L0_conv_proj_b, L0_conv_skip_scale)
    x = x + _L1_conv_ref(_gn(x), L1_conv_wg, L1_conv_wg1, L1_conv_g_gamma, L1_conv_g_beta, L1_conv_g_mean, L1_conv_g_var, L1_conv_g1_gamma, L1_conv_g1_beta, L1_conv_g1_mean, L1_conv_g1_var, L1_conv_out_gamma, L1_conv_out_beta, L1_conv_out_mean, L1_conv_out_var)
    return x


_drawn_inputs = setup_inputs


def setup_inputs(seed=0):
    import zlib

    import numpy as np

    out = dict(_drawn_inputs(seed))
    spreads = {'L0_conv_ln_g': (1.0, 0.2),
     'L0_conv_ln_b': (0.0, 0.1),
     'L0_conv_conv_b': (0.0, 0.8),
     'L0_conv_D': (1.0, 0.6),
     'L0_conv_proj_b': (0.0, 0.1)}
    factors = {'L0_conv_in_proj_w': 8.0,
     'L0_conv_conv_w': 8.0,
     'L0_conv_x_proj_w': 8.0,
     'L0_conv_dt_proj_w': 8.0,
     'L0_conv_dt_proj_b': 8.0,
     'L0_conv_A_log': 8.0,
     'L0_conv_out_proj_w': 8.0,
     'L1_conv_g_gamma': 8.0,
     'L1_conv_g_beta': 3.435,
     'L1_conv_g_mean': 3.177,
     'L1_conv_g_var': 4.435,
     'L1_conv_g1_gamma': 8.0,
     'L1_conv_g1_beta': 3.21,
     'L1_conv_g1_mean': 3.208,
     'L1_conv_g1_var': 5.638}
    for name, (base, spread) in spreads.items():
        noise = np.random.default_rng([zlib.crc32(name.encode()), seed]).standard_normal(out[name].shape)
        drawn = base * np.exp(spread * noise) if base else spread * noise
        out[name] = jnp.asarray(drawn.astype(out[name].dtype))
    for name, factor in factors.items():
        out[name] = (out[name] * factor).astype(out[name].dtype)
    return out
```

```python
import numpy as np
import concourse.bass as bass
from concourse import mybir
from contextlib import ExitStack

F32 = mybir.dt.float32
BF16 = mybir.dt.bfloat16
U8 = mybir.dt.uint8
ALU = mybir.AluOpType
ACT = mybir.ActivationFunctionType

P = 128
T = 512
LEAD = 2
GN_EPS0, LN_EPS = 1e-5, 1e-5
GROUPS = 32
SERIES_BELOW = 2.0 ** -6


class Signal:

    def __init__(self, sem, per):
        self.sem, self.per = sem, per

    def of(self, t, k):
        return t * self.per + (LEAD * self.per + k)


def token_mixer(nc, a, debug=False):
    x = a["x"]
    B, H, W, C = x.shape
    L = H * W
    NCH = L // T
    Q = T // P
    KC = C // P
    DI = a["in_proj_wT"].shape[1] // 2
    KD = DI // P
    N = a["A_log"].shape[1]
    R = a["dt_proj_wT"].shape[0]
    DT0 = 3 * 2 * N
    TAPS = a["conv_w"].shape[1]
    HALO = TAPS - 1
    CG = C // GROUPS
    assert T % P == 0 and KC == 2 and KD == 4 and N == 16 and NCH >= 4 and NCH % 2 == 0

    x_tok = x.rearrange("b h w c -> b (h w) c")
    ctx = ExitStack()
    with ctx:
        def sb(name, shape, dt=F32):
            return ctx.enter_context(nc.sbuf_tensor(name, shape, dt))

        def signal(name, per):
            s = Signal(ctx.enter_context(nc.semaphore(name)), per)
            signals.append(s)
            return s

        def sem(name):
            return ctx.enter_context(nc.semaphore(name))

        signals = []
        x1_dram = a["x1_dram"]

        ident = sb("ident", [P, P])
        minus_half = sb("minus_half", [P, GROUPS])
        x1_mv = sb("x1_mv", [P, 2, B])
        all_layers, ctx = ctx, ExitStack()
        avg_all = sb("avg_all", [P, P])
        select = sb("select", [DT0, 2 * N, P], BF16)
        in_w = sb("in_w", [P, KC, 2 * DI])
        xp_w = sb("xp_w", [P, KD, DT0 + R])
        dt_w = sb("dt_w", [P, DI])
        out_w = sb("out_w", [P, KD, C])
        proj_w = sb("proj_w", [P, KC, C])
        conv_w = sb("conv_w", [P, KD, TAPS])
        conv_b = sb("conv_b", [P, KD])
        dt_b = sb("dt_b", [P, KD])
        skip_D = sb("skip_D", [P, KD])
        a_log = sb("a_log", [P, KD, N])
        decay = sb("decay", [P, KD, N])
        ln_g = sb("ln_g", [P, KC])
        ln_b = sb("ln_b", [P, KC])
        proj_b = sb("proj_b", [P, KC])
        skip_s = sb("skip_s", [P, 1])
        skip_ident = sb("skip_ident", [P, P])
        zeros = sb("zeros", [P, KD * N])
        gn_scale = sb("gn_scale", [P, B, GROUPS])
        gn_shift = sb("gn_shift", [P, B, GROUPS])

        loaded = sem("weights_loaded")
        loads = [(ident[:], a["ident"]), (avg_all[:], a["avg_all"]), (select[:].bitcast(mybir.dt.uint16), a["select"]),
                 (in_w[:], a["in_proj_wT"].rearrange("(k p) m -> p k m", p=P)),
                 (dt_w[DT0:DT0 + R, :], a["dt_proj_wT"]),
                 (out_w[:], a["out_proj_wT"].rearrange("(k p) m -> p k m", p=P)),
                 (proj_w[:], a["proj_wT"].rearrange("(k p) m -> p k m", p=P)),
                 (conv_w[:], a["conv_w"].rearrange("(k p) m -> p k m", p=P)),
                 (a_log[:], a["A_log"].rearrange("(k p) m -> p k m", p=P)),
                 (conv_b[:], a["conv_b"]),
                 (dt_b[:], a["dt_proj_b"]),
                 (skip_D[:], a["D"]),
                 (ln_g[:], a["ln_g"]),
                 (ln_b[:], a["ln_b"]),
                 (proj_b[:], a["proj_b"]),
                 (skip_s[:], a["skip_scale"].partition_broadcast(P))]
        xp_T = a["x_proj_wT"].rearrange("(k p) m -> p k m", p=P)
        loads += [(xp_w[:, :, 2 * N * i:2 * N * (i + 1)], xp_T[:, :, R:R + 2 * N]) for i in range(3)]
        loads += [(xp_w[:, :, DT0:DT0 + R], xp_T[:, :, 0:R])]

        SQ = 16
        while (L // (P * SQ)) < 1 or L % (P * SQ):
            SQ //= 2
        NT = L // (P * SQ)
        x_stat = x.rearrange("b h w c -> (b h w) c").rearrange("(n p q) c -> n p q c", p=P, q=SQ)
        with (
            nc.sbuf_tensor("stat_x", [P, 2, SQ, C], F32) as stat_x,
            nc.sbuf_tensor("stat_bn", [P, GROUPS, NT, 6], F32) as stat_bn,
            nc.sbuf_tensor("stat_mv", [P, 2, GROUPS], F32) as stat_mv,
            nc.sbuf_tensor("stat_diff", [P, GROUPS], F32) as stat_diff,
            nc.sbuf_tensor("stat_mean", [P, GROUPS], F32) as stat_mean,
            nc.sbuf_tensor("stat_rstd", [P, GROUPS], F32) as stat_rstd,
            nc.psum_tensor("stat_psum", [P, 2, 512], F32) as stat_psum,
            nc.semaphore("stat_loaded0") as stat_loaded0,
            nc.semaphore("stat_loaded1") as stat_loaded1,
            nc.semaphore("stat_tile_done") as stat_tile_done,
            nc.semaphore("stat_step") as stat_step,
            nc.semaphore("stat_averaged") as stat_averaged,
            nc.semaphore("stat_pow") as stat_pow,
            nc.semaphore("const_ready") as const_ready,
            nc.semaphore("act_ready") as act_ready,
            nc.Block() as block,
        ):
            stat_loaded = [stat_loaded0, stat_loaded1]
            steps_per_batch = 7

            @block.sync
            def _(sp):
                for dst, src in loads:
                    sp.dma_start(dst, src).then_inc(loaded, 16)
                for b in range(B):
                    for n in range(NT):
                        i = b * NT + n
                        if i >= 2:
                            sp.wait_ge(stat_tile_done, i - 1)
                        sp.dma_start(stat_x[:, i % 2], x_stat[i]).then_inc(stat_loaded[i % 2], 16)

            @block.vector
            def _(dve):
                nc.vector.memset(zeros[:], 0.0)
                nc.vector.memset(minus_half[:], -0.5).then_inc(const_ready, 1)
                for b in range(B):
                    for n in range(NT):
                        i = b * NT + n
                        dve.wait_ge(stat_loaded[i % 2], 16 * (i // 2 + 1))
                        for g in range(GROUPS):
                            last = nc.vector.bn_stats(stat_bn[:, g, n, :], stat_x[:, i % 2, :, g * CG:(g + 1) * CG])
                        last.then_inc(stat_tile_done, 1)
                    done = b * steps_per_batch
                    dve.wait_ge(stat_tile_done, (b + 1) * NT)
                    if b:
                        dve.wait_ge(stat_averaged, 2 * b)
                    for g in range(GROUPS):
                        last = nc.vector.bn_aggr(stat_mv[:, :, g], stat_bn[:, g, :, :])
                    last.then_inc(stat_step, 1)
                    dve.wait_ge(stat_averaged, 2 * b + 1)
                    nc.vector.tensor_copy(stat_mean[:], stat_psum[:, 0, 0:GROUPS]).then_inc(stat_step, 1)
                    dve.wait_ge(stat_step, done + 2)
                    nc.vector.tensor_tensor(stat_diff[:], stat_mv[:, 0, :], stat_mean[:], ALU.subtract).then_inc(stat_step, 1)
                    dve.wait_ge(stat_step, done + 3)
                    nc.vector.tensor_tensor(stat_diff[:], stat_diff[:], stat_diff[:], ALU.mult).then_inc(stat_step, 1)
                    dve.wait_ge(stat_step, done + 4)
                    nc.vector.tensor_tensor(stat_diff[:], stat_diff[:], stat_mv[:, 1, :], ALU.add).then_inc(stat_step, 1)
                    dve.wait_ge(stat_averaged, 2 * b + 2)
                    if b:
                        dve.wait_ge(stat_pow, b)
                    nc.vector.tensor_scalar(stat_rstd[:], stat_psum[:, 1, 0:GROUPS], GN_EPS0, None, ALU.add).then_inc(stat_step, 1)
                    dve.wait_ge(stat_pow, b + 1)
                    nc.vector.tensor_copy(gn_scale[:, b, :], stat_rstd[:])
                    nc.vector.scalar_tensor_tensor(gn_shift[:, b, :], stat_mean[:], -1.0, stat_rstd[:],
                                                   ALU.mult, ALU.mult).then_inc(stat_step, 1)

            @block.tensor
            def _(pe):
                pe.wait_ge(loaded, 16 * len(loads))
                for b in range(B):
                    pe.wait_ge(stat_step, b * steps_per_batch + 1)
                    nc.tensor.matmul(stat_psum[:, 0, 0:GROUPS], avg_all[:], stat_mv[:, 0, :],
                                     start=True, stop=True).then_inc(stat_averaged, 1)
                    pe.wait_ge(stat_step, b * steps_per_batch + 5)
                    nc.tensor.matmul(stat_psum[:, 1, 0:GROUPS], avg_all[:], stat_diff[:],
                                     start=True, stop=True).then_inc(stat_averaged, 1)

            @block.gpsimd
            def _(pool):
                pool.wait_ge(const_ready, 1)
                for b in range(B):
                    pool.wait_ge(stat_step, b * steps_per_batch + 6)
                    nc.gpsimd.tensor_tensor(stat_rstd[:], stat_rstd[:], minus_half[:], ALU.pow).then_inc(stat_pow, 1)

            @block.scalar
            def _(act):
                act.wait_ge(loaded, 16 * len(loads))
                nc.scalar.activation(decay[:], a_log[:], ACT.Exp).then_inc(act_ready, 1)
                nc.scalar.activation(skip_ident[:], ident[:], ACT.Copy, scale=skip_s[:, 0:1])
                act.wait_ge(act_ready, 1)
                nc.scalar.mul(decay[:], decay[:], -1.0)

        with ExitStack() as layer0:
            mixer_layer(nc, a, layer0, locals())
        ctx.close()
        if not debug:
            with ExitStack() as layer1:
                diffusion_layer(nc, a, layer1, ident, minus_half, x1_mv, B, H, W, C)


def mixer_layer(nc, a, ctx, env):
    (B, L, NCH, Q, KC, C, DI, KD, N, R, DT0, TAPS, HALO, x_tok, x1_dram) = (
        env[k] for k in "B L NCH Q KC C DI KD N R DT0 TAPS HALO x_tok x1_dram".split())
    (ident, select, in_w, xp_w, dt_w, out_w, proj_w, conv_w, conv_b, dt_b, skip_D, decay, ln_g, ln_b,
     proj_b, skip_ident, zeros, minus_half, gn_scale, gn_shift, x1_mv) = (
        env[k] for k in ("ident select in_w xp_w dt_w out_w proj_w conv_w conv_b dt_b skip_D decay ln_g ln_b "
                         "proj_b skip_ident zeros minus_half gn_scale gn_shift x1_mv").split())

    def sb(name, shape, dt=F32):
        return ctx.enter_context(nc.sbuf_tensor(name, shape, dt))

    signals = []

    def signal(name, per):
        s = Signal(ctx.enter_context(nc.semaphore(name)), per)
        signals.append(s)
        return s

    xt = sb("xt", [P, Q, C])
    gy = sb("gy", [P, Q, C])
    gn_now = sb("gn_now", [P, 2, 32])
    eps = sb("eps", [P, Q])
    held = sb("held", [P, 2])
    bn1 = sb("bn1", [P, Q, 6])
    mv1 = sb("mv1", [P, Q, 2])
    rstd1 = sb("rstd1", [P, Q])
    xnT = sb("xnT", [P, 2, KC, T])
    xi = sb("xi", [P, KD, HALO + T])
    zs = sb("zs", [P, 2, KD, T])
    xs = sb("xs", [P, 2, KD, T])
    ta = sb("ta", [P, KD, T])
    tb = sb("tb", [P, KD, T])
    large = sb("large", [P, KD, T], U8)
    delta = sb("delta", [P, 2, KD, T])
    du = sb("du", [P, 2, KD, T])
    dtT = sb("dtT", [P, T])
    bc_high = sb("bc_high", [DT0, T], BF16)
    bc_mid = bc_high
    bc_rest = dtT[0:DT0, :]
    bc3 = sb("bc3", [DT0, 2, T], BF16)
    dA = sb("dA", [P, 2, KD, T + 1])
    hh = sb("hh", [P, 2, KD, T + 1])
    hc = sb("hc", [P, 2, KD, T])
    carry = sb("carry", [P, N, KD])
    xr = sb("xr", [P, Q, C])
    z2 = sb("z2", [P, Q, C])
    bn2 = sb("bn2", [P, Q, 6])
    mv2 = sb("mv2", [P, Q, 2])
    rstd2 = sb("rstd2", [P, Q])
    z2T = sb("z2T", [P, KC, T])
    x1 = sb("x1", [P, KC, T])

    x1_bn = sb("x1_bn", [P, 2 * NCH, 6])
    x1_batch = sb("x1_batch", [P, 2])

    y_ps = ctx.enter_context(nc.psum_tensor("y_ps", [P, KD, T], F32))
    B_ps = ctx.enter_context(nc.psum_tensor("B_ps", [P, T], F32))
    C_ps = ctx.enter_context(nc.psum_tensor("C_ps", [P, T], F32))
    G = ctx.enter_context(nc.psum_tensor("G", [P, 2, T], F32))

    x_loaded = signal("x_loaded", 16)
    gn_scaled = signal("gn_scaled", 1)
    gn_done = signal("gn_done", 1)
    ln1_stats = signal("ln1_stats", 1)
    ln1_mv = signal("ln1_mv", 1)
    ln1_eps = signal("ln1_eps", 1)
    ln1_rstd = signal("ln1_rstd", 1)
    ln1_norm = signal("ln1_norm", 1)
    xn_T = signal("xn_T", 1)
    xn_evac = signal("xn_evac", 2)
    xz_mm = signal("xz_mm", 2 * KD)
    halo_moved = signal("halo_moved", 1)
    xz_evac = signal("xz_evac", 2 * KD)
    conv_step = signal("conv_step", KD * TAPS)
    xs_done = signal("xs_done", KD)
    xdbl_mm = signal("xdbl_mm", 1)
    dt_evac = signal("dt_evac", 1)
    bc_split = signal("bc_split", 1)
    bc_step = signal("bc_step", 3)
    bc_mid_done = signal("bc_mid_done", 2)
    dtp_mm = signal("dtp_mm", KD)
    dtp_evac = signal("dtp_evac", KD)
    sp_exp = signal("sp_exp", 1)
    sp_ln = signal("sp_ln", 1)
    series = signal("series", 4)
    chosen = signal("chosen", 2)
    delta_done = signal("delta_done", 1)
    du_done = signal("du_done", 1)
    dA_ready = signal("dA_ready", N)
    carry_loaded = signal("carry_loaded", N)
    carry_saved = signal("carry_saved", N)
    carry_zeroed = signal("carry_zeroed", 1)
    B_ready = signal("B_ready", N)
    C_ready = signal("C_ready", N)
    dBu_done = signal("dBu_done", N)
    scan_done = signal("scan_done", N)
    hC_done = signal("hC_done", N)
    y_acc = signal("y_acc", N)
    y_evac = signal("y_evac", KD)
    yg_done = signal("yg_done", 1)
    outp_mm = signal("outp_mm", Q)
    ln2_stats = signal("ln2_stats", 1)
    ln2_mv = signal("ln2_mv", 1)
    ln2_eps = signal("ln2_eps", 1)
    ln2_rstd = signal("ln2_rstd", 1)
    ln2_norm = signal("ln2_norm", 1)
    z2_T = signal("z2_T", 1)
    z2_evac = signal("z2_evac", 2)
    xr_loaded = signal("xr_loaded", 16)
    x1_mm = signal("x1_mm", 2)
    x1_evac = signal("x1_evac", 2)
    x1_stored = signal("x1_stored", 16)
    x1_stats = signal("x1_stats", 1)
    x1_total = ctx.enter_context(nc.semaphore("x1_total"))
    gn_batch = ctx.enter_context(nc.semaphore("gn_batch"))
    zeroed = ctx.enter_context(nc.semaphore("zeroed"))

    block = ctx.enter_context(nc.Block())

    def batch(eng, front, period, back):
        with eng.Fori(0, B) as b:
            t0 = b * NCH
            front(b, 0, t0, 0, alone=True)
            period(b, 0, t0, 0, has_back=False, has_front=True)
            with eng.Fori(0, NCH // 2 - 1) as i:
                period(b, i * 2 + 1, t0 + i * 2 + 1, 1, has_back=True, has_front=True)
                period(b, i * 2 + 2, t0 + i * 2 + 2, 0, has_back=True, has_front=True)
            period(b, NCH - 1, t0 + NCH - 1, 1, has_back=True, has_front=False)
            back(b, NCH - 1, t0 + NCH - 1, 1)

    def wait(eng, sig, t, k):
        eng.wait_ge(sig.sem, sig.of(t, k))

    @block.sync
    def _(sp):
        for s in signals:
            sp.sem_inc(s.sem, LEAD * s.per)

        def front(b, j, t, par, alone=False):
            wait(sp, gn_scaled, t - 1, 1)
            sp.dma_start(xt[:], x_tok[b, bass.ds(j * T, T), :].rearrange("(q p) c -> p q c", p=P)
                         ).then_inc(x_loaded.sem, 16)

        def load_residual(b, j, t):
            wait(sp, x1_mm, t - 1, 2)
            sp.dma_start(xr[:], x_tok[b, bass.ds(j * T, T), :].rearrange("(q p) c -> p q c", p=P)
                         ).then_inc(xr_loaded.sem, 16)

        def store(b, j, t):
            wait(sp, x1_evac, t, 2)
            sp.dma_start(x1_dram[b, :, :, bass.ds(j * T, T)].rearrange("k p t -> p k t"), x1[:]
                         ).then_inc(x1_stored.sem, 16)

        def period(b, j, t, par, has_back, has_front):
            if has_back:
                load_residual(b, j - 1, t - 1)
            if has_front:
                front(b, j + 1, t + 1, 1 - par)
            if has_back:
                store(b, j - 1, t - 1)

        def back(b, j, t, par):
            load_residual(b, j, t)
            store(b, j, t)

        batch(sp, front, period, back)
        wait(sp, x1_stored, B * NCH - 1, 16)

    @block.gpsimd
    def _(pool):
        nc.gpsimd.memset(eps[:], LN_EPS)
        nc.gpsimd.memset(dA[:, :, :, 0:1], 0.0).then_inc(zeroed, 1)
        pool.wait_ge(zeroed, 1)

        def rstd(t, mv, out, got_mv, eps_added, done):
            wait(pool, got_mv, t, 1)
            nc.gpsimd.tensor_tensor(out[:], mv[:, :, 1], eps[:], ALU.add).then_inc(eps_added.sem, 1)
            wait(pool, eps_added, t, 1)
            nc.gpsimd.tensor_tensor(out[:], out[:], minus_half[:, 0:Q], ALU.pow).then_inc(done.sem, 1)

        def groups(tile):
            return tile[:].rearrange("p q (g c) -> p q g c", g=GROUPS)

        def per_group(tile):
            return tile.unsqueeze(3).broadcast_to([P, Q, GROUPS, C // GROUPS])

        def front_norm(b, t):
            wait(pool, x_loaded, t, 16)
            wait(pool, xn_T, t - 1, 1)
            nc.gpsimd.tensor_tensor(groups(gy), groups(xt), per_group(gn_now[:, 0:1]),
                                    ALU.mult).then_inc(gn_scaled.sem, 1)
            wait(pool, gn_scaled, t, 1)
            nc.gpsimd.tensor_tensor(groups(gy), groups(gy), per_group(gn_now[:, 1:2]),
                                    ALU.add).then_inc(gn_done.sem, 1)
            rstd(t, mv1, rstd1, ln1_mv, ln1_eps, ln1_rstd)

        def front_series(t, par):
            e = du[:, par]
            for k, (other, op) in enumerate(((e, ALU.mult), (e, ALU.mult), (e, ALU.add))):
                wait(pool, series, t, k + 1)
                nc.gpsimd.tensor_tensor(ta[:], ta[:], other, op).then_inc(series.sem, 1)
            wait(pool, chosen, t, 2)
            nc.gpsimd.tensor_tensor(delta[:, par], delta[:, par], ta[:], ALU.add).then_inc(delta_done.sem, 1)
            wait(pool, delta_done, t, 1)
            nc.gpsimd.tensor_tensor(du[:, par], delta[:, par], xs[:, par], ALU.mult).then_inc(du_done.sem, 1)

        def front(b, j, t, par, alone=False):
            nc.gpsimd.tensor_copy(gn_now[:, 0:1, :], gn_scale[:, bass.ds(b, 1), :])
            nc.gpsimd.tensor_copy(gn_now[:, 1:2, :], gn_shift[:, bass.ds(b, 1), :]).then_inc(gn_batch, 1)
            pool.wait_ge(gn_batch, b + 1)
            front_norm(b, t)
            front_series(t, par)

        def gate(t, par):
            wait(pool, y_evac, t, KD)
            nc.gpsimd.tensor_tensor(xs[:, par], xs[:, par], zs[:, par], ALU.mult).then_inc(yg_done.sem, 1)

        def period(b, j, t, par, has_back, has_front):
            if has_front:
                front_norm(b, t + 1)
            if has_back:
                rstd(t - 1, mv2, rstd2, ln2_mv, ln2_eps, ln2_rstd)
            if has_front:
                front_series(t + 1, 1 - par)
            gate(t, par)

        def back(b, j, t, par):
            rstd(t, mv2, rstd2, ln2_mv, ln2_eps, ln2_rstd)

        batch(pool, front, period, back)

    @block.scalar
    def _(act):
        act.wait_ge(zeroed, 1)

        def scan_step(t, par, n):
            buf = n % 2
            if n == 0:
                wait(act, delta_done, t, 1)
            if n >= 2:
                wait(act, scan_done, t, n - 1)
            else:
                wait(act, scan_done, t - 1, N - 1 + n)
            for m in range(KD):
                last = nc.scalar.activation(dA[:, buf, m, 1:T + 1], delta[:, par, m], ACT.Exp,
                                            scale=decay[:, m, n:n + 1])
            last.then_inc(dA_ready.sem, 1)
            if n >= 2:
                wait(act, hC_done, t, n - 1)
                wait(act, carry_saved, t, n - 1)
            else:
                wait(act, hC_done, t - 1, N - 1 + n)
                wait(act, carry_saved, t - 1, N - 1 + n)
            nc.scalar.copy(hh[:, buf, :, 0], carry[:, n, :]).then_inc(carry_loaded.sem, 1)
            if n:
                save_carry(t, n - 1)

        def save_carry(t, n):
            wait(act, scan_done, t, n + 1)
            wait(act, carry_loaded, t, n + 1)
            nc.scalar.copy(carry[:, n, :], hh[:, n % 2, :, T]).then_inc(carry_saved.sem, 1)

        def front_xn(t, par):
            wait(act, xn_T, t, 1)
            for k in range(KC):
                nc.scalar.activation(xnT[:, par, k], G[:, k], ACT.Identity, bias=ln_b[:, k:k + 1],
                                     scale=ln_g[:, k:k + 1]).then_inc(xn_evac.sem, 1)

        def front_halo(t, first):
            wait(act, conv_step, t - 1, KD * TAPS)
            wait(act, xz_evac, t - 1, KD)
            if first:
                nc.scalar.copy(xi[:, :, 0:HALO], zeros[:, 0:KD * HALO].rearrange("p (k h) -> p k h", h=HALO)
                               ).then_inc(halo_moved.sem, 1)
            else:
                nc.scalar.copy(xi[:, :, 0:HALO], xi[:, :, T:T + HALO]).then_inc(halo_moved.sem, 1)

        def front_xz(t, par, m0, m1):
            if m0 == 0:
                wait(act, halo_moved, t, 1)
            for m in range(m0, m1):
                wait(act, xz_mm, t, m + 1)
                if m < KD:
                    nc.scalar.copy(xi[:, m, HALO:], G[:, m % 2]).then_inc(xz_evac.sem, 1)
                else:
                    nc.scalar.activation(zs[:, par, m - KD], G[:, m % 2], ACT.Silu).then_inc(xz_evac.sem, 1)

        def front_silu(t, par):
            wait(act, outp_mm, t - 2, Q)
            for m in range(KD):
                wait(act, conv_step, t, KD * (TAPS - 1) + m + 1)
                nc.scalar.activation(xs[:, par, m], ta[:, m], ACT.Silu).then_inc(xs_done.sem, 1)

        def front_bc(t, par):
            wait(act, xdbl_mm, t, 1)
            nc.scalar.copy(dtT[DT0:DT0 + R, :], G[DT0:DT0 + R, 0]).then_inc(dt_evac.sem, 1)
            nc.scalar.copy(bc3[0:2 * N, par], G[0:2 * N, 0])
            nc.scalar.copy(bc_high[:], G[0:DT0, 0]).then_inc(bc_split.sem, 1)

        def front_softplus(t, par):
            for m in range(KD):
                wait(act, dtp_mm, t, m + 1)
                v = G[:, (m + 1) % 2]
                nc.scalar.activation(du[:, par, m], v, ACT.Abs, bias=dt_b[:, m:m + 1])
                nc.scalar.activation(delta[:, par, m], v, ACT.Relu, bias=dt_b[:, m:m + 1]).then_inc(dtp_evac.sem, 1)
            wait(act, dtp_evac, t, KD)
            nc.scalar.activation(du[:, par], du[:, par], ACT.Exp, scale=-1.0).then_inc(sp_exp.sem, 1)
            wait(act, sp_exp, t, 1)
            nc.scalar.activation(ta[:], du[:, par], ACT.Copy, bias=-0.5, scale=1.0 / 3).then_inc(series.sem, 1)
            wait(act, chosen, t - 1, 2)
            nc.scalar.activation(tb[:], du[:, par], ACT.Ln, bias=1.0).then_inc(sp_ln.sem, 1)

        def back_z2(t):
            wait(act, z2_T, t, 1)
            for k in range(KC):
                nc.scalar.activation(z2T[:, k], G[:, k], ACT.Identity, bias=ln_b[:, k:k + 1],
                                     scale=ln_g[:, k:k + 1]).then_inc(z2_evac.sem, 1)

        def back_x1(t):
            wait(act, x1_stored, t - 1, 16)
            wait(act, x1_stats, t - 1, 1)
            for k in range(KC):
                wait(act, x1_mm, t, k + 1)
                nc.scalar.activation(x1[:, k], G[:, k], ACT.Identity, bias=proj_b[:, k:k + 1]
                                     ).then_inc(x1_evac.sem, 1)

        def front(b, j, t, par, alone=False):
            wait(act, carry_saved, t - 1, N)
            nc.scalar.copy(carry[:].rearrange("p n k -> p (n k)"), zeros[:]).then_inc(carry_zeroed.sem, 1)
            act.wait_ge(carry_zeroed.sem, b + (LEAD + 1))
            front_xn(t, par)
            front_halo(t, True)
            front_xz(t, par, 0, 2 * KD)
            front_silu(t, par)
            front_bc(t, par)
            front_softplus(t, par)

        def period(b, j, t, par, has_back, has_front):
            for n in range(N):
                scan_step(t, par, n)
                if has_front:
                    f, fp = t + 1, 1 - par
                    if n == 3:
                        front_xn(f, fp)
                        front_halo(f, False)
                    if n == 4:
                        front_xz(f, fp, 0, 3)
                    if n == 5:
                        front_xz(f, fp, 3, 6)
                    if n == 6:
                        front_xz(f, fp, 6, 8)
                    if n == 8:
                        front_silu(f, fp)
                        front_bc(f, fp)
                    if n == 9:
                        front_softplus(f, fp)
                if has_back and n == 11:
                    back_z2(t - 1)
                if has_back and n == 12:
                    back_x1(t - 1)
            save_carry(t, N - 1)

        def back(b, j, t, par):
            back_z2(t)
            back_x1(t)

        batch(act, front, period, back)

    @block.vector
    def _(dve):
        def scan_step(t, par, n):
            buf = n % 2
            if n == 0:
                wait(dve, du_done, t, 1)
            wait(dve, B_ready, t, n + 1)
            if n >= 2:
                wait(dve, carry_saved, t, n - 1)
                wait(dve, hC_done, t, n - 1)
            else:
                wait(dve, carry_saved, t - 1, N - 1 + n)
                wait(dve, hC_done, t - 1, N - 1 + n)
            nc.vector.tensor_tensor(hh[:, buf, :, 1:T + 1], du[:, par],
                                    B_ps[:].unsqueeze(1).broadcast_to([P, KD, T]), ALU.mult).then_inc(dBu_done.sem, 1)
            wait(dve, dA_ready, t, n + 1)
            wait(dve, carry_loaded, t, n + 1)
            wait(dve, dBu_done, t, n + 1)
            states = hh[:, buf].rearrange("p k t -> p (k t)")
            nc.vector.tensor_tensor_scan(states, dA[:, buf].rearrange("p k t -> p (k t)"), states, 0.0,
                                         ALU.mult, ALU.add).then_inc(scan_done.sem, 1)
            wait(dve, C_ready, t, n + 1)
            wait(dve, scan_done, t, n + 1)
            if n >= 2:
                wait(dve, y_acc, t, n - 1)
            else:
                wait(dve, y_acc, t - 1, N - 1 + n)
            nc.vector.tensor_tensor(hc[:, buf], hh[:, buf, :, 1:T + 1],
                                    C_ps[:].unsqueeze(1).broadcast_to([P, KD, T]), ALU.mult).then_inc(hC_done.sem, 1)

        def hold():
            nc.vector.memset(held[:, 0:1], 0.0)

        def moments(t, src, bn, mv, stats, got_mv):
            for q in range(Q):
                last = nc.vector.bn_stats(bn[:, q, :], src(q))
            last.then_inc(stats.sem, 1)
            wait(dve, stats, t, 1)
            hold()
            for q in range(Q):
                last = nc.vector.bn_aggr(mv[:, q, :], bn[:, q, :])
            last.then_inc(got_mv.sem, 1)

        def front_moments(t):
            wait(dve, gn_done, t, 1)
            moments(t, lambda q: gy[:, q, :], bn1, mv1, ln1_stats, ln1_mv)

        def front_norm(t):
            wait(dve, ln1_rstd, t, 1)
            for q in range(Q):
                last = nc.vector.tensor_scalar(gy[:, q, :], gy[:, q, :], mv1[:, q, 0:1], rstd1[:, q:q + 1],
                                               ALU.subtract, ALU.mult)
            last.then_inc(ln1_norm.sem, 1)

        def front_conv(t):
            wait(dve, delta_done, t - 1, 1)
            for m in range(KD):
                wait(dve, xz_evac, t, m + 1)
                nc.vector.tensor_scalar(ta[:, m], xi[:, m, 0:T], conv_w[:, m, 0:1], conv_b[:, m:m + 1],
                                        ALU.mult, ALU.add).then_inc(conv_step.sem, 1)
            for tap in range(1, TAPS):
                for m in range(KD):
                    wait(dve, conv_step, t, KD * (tap - 1) + m + 1)
                    nc.vector.scalar_tensor_tensor(ta[:, m], xi[:, m, tap:tap + T], conv_w[:, m, tap:tap + 1],
                                                   ta[:, m], ALU.mult, ALU.add).then_inc(conv_step.sem, 1)

        def front_bc(t, par):
            wait(dve, bc_split, t, 1)
            nc.vector.tensor_tensor(bc_rest, G[0:DT0, 0], bc_high[:], ALU.subtract).then_inc(bc_step.sem, 1)
            wait(dve, bc_step, t, 1)
            nc.vector.tensor_copy(bc_mid[:], bc_rest).then_inc(bc_step.sem, 1)
            nc.vector.tensor_copy(bc3[2 * N:4 * N, par], dtT[2 * N:4 * N, :])
            wait(dve, bc_step, t, 2)
            nc.vector.tensor_tensor(bc3[4 * N:6 * N, par], dtT[4 * N:6 * N, :], bc_mid[4 * N:6 * N, :],
                                    ALU.subtract).then_inc(bc_step.sem, 1)

        def front_choose(t, par):
            wait(dve, sp_exp, t, 1)
            nc.vector.tensor_scalar(large[:], du[:, par], SERIES_BELOW, None, ALU.is_ge).then_inc(chosen.sem, 1)
            wait(dve, chosen, t, 1)
            wait(dve, sp_ln, t, 1)
            wait(dve, series, t, 4)
            hold()
            nc.vector.copy_predicated(ta[:], large[:], tb[:]).then_inc(chosen.sem, 1)

        def y_out(t, par):
            wait(dve, y_acc, t, N)
            for m in range(KD):
                nc.vector.scalar_tensor_tensor(xs[:, par, m], xs[:, par, m], skip_D[:, m:m + 1], y_ps[:, m],
                                               ALU.mult, ALU.add).then_inc(y_evac.sem, 1)

        def back_moments(t):
            wait(dve, outp_mm, t, Q)
            moments(t, lambda q: G[:, q // 2, (q % 2) * C:(q % 2 + 1) * C], bn2, mv2, ln2_stats, ln2_mv)

        def back_norm(t):
            wait(dve, ln2_rstd, t, 1)
            wait(dve, z2_T, t - 1, 1)
            for q in range(Q):
                last = nc.vector.tensor_scalar(z2[:, q, :], G[:, q // 2, (q % 2) * C:(q % 2 + 1) * C],
                                               mv2[:, q, 0:1], rstd2[:, q:q + 1], ALU.subtract, ALU.mult)
            last.then_inc(ln2_norm.sem, 1)

        def back_stats(j, t):
            wait(dve, x1_evac, t, 2)
            for k in range(KC):
                last = nc.vector.bn_stats(x1_bn[:, bass.ds(j * 2 + k, 1), :], x1[:, k])
            last.then_inc(x1_stats.sem, 1)

        def front(b, j, t, par, alone=False):
            front_moments(t)
            front_norm(t)
            front_conv(t)
            front_bc(t, par)
            front_choose(t, par)

        def period(b, j, t, par, has_back, has_front):
            for n in range(N):
                scan_step(t, par, n)
                f, fp = t + 1, 1 - par
                if has_back and n == 1:
                    back_moments(t - 1)
                if has_back and n == 2:
                    back_norm(t - 1)
                if has_back and n == 13:
                    back_stats(j - 1, t - 1)
                if has_front:
                    if n == 1:
                        front_moments(f)
                    if n == 2:
                        front_norm(f)
                    if n == 7:
                        front_conv(f)
                    if n == 8:
                        front_bc(f, fp)
                    if n == 12:
                        front_choose(f, fp)
            y_out(t, par)

        def back(b, j, t, par):
            back_moments(t)
            back_norm(t)
            back_stats(j, t)
            wait(dve, x1_stats, t, 1)
            hold()
            nc.vector.bn_aggr(x1_batch[:], x1_bn[:].rearrange("p n s -> p (n s)")).then_inc(x1_total, 1)
            dve.wait_ge(x1_total, b * 2 + 1)
            nc.vector.tensor_copy(x1_mv[:, :, bass.ds(b, 1)], x1_batch[:].unsqueeze(2)).then_inc(x1_total, 1)
            dve.wait_ge(x1_total, b * 2 + 2)

        batch(dve, front, period, back)

    @block.tensor
    def _(pe):
        def spread(t, par, n):
            if n == 0:
                wait(pe, bc_step, t, 3)
            wait(pe, dBu_done, t, n)
            nc.tensor.matmul(B_ps[:], select[:, n, :], bc3[:, par], start=True, stop=True).then_inc(B_ready.sem, 1)
            wait(pe, hC_done, t, n)
            nc.tensor.matmul(C_ps[:], select[:, N + n, :], bc3[:, par], start=True, stop=True).then_inc(C_ready.sem, 1)

        def add_y(t, n):
            if n == 0:
                wait(pe, y_evac, t - 1, KD)
            wait(pe, hC_done, t, n + 1)
            for m in range(KD):
                last = nc.tensor.matmul(y_ps[:, m], ident[:], hc[:, n % 2, m], start=(n == 0), stop=(n == N - 1))
            last.then_inc(y_acc.sem, 1)

        def front_T(t, first, after_front):
            wait(pe, ln1_norm, t, 1)
            if first:
                wait(pe, x1_evac, t - 1, 2)
            elif after_front:
                wait(pe, dtp_evac, t - 1, KD)
            else:
                wait(pe, ln2_norm, t - 2, 1)
            for k in range(KC):
                for q in range(Q):
                    last = nc.tensor.transpose(G[:, k, q * P:(q + 1) * P], gy[:, q, k * P:(k + 1) * P], ident[:])
            last.then_inc(xn_T.sem, 1)

        def front_xz(t, par, m0, m1):
            for m in range(m0, m1):
                if m < 2:
                    wait(pe, xn_evac, t, 2)
                else:
                    wait(pe, xz_evac, t, m - 1)
                for k in range(KC):
                    last = nc.tensor.matmul(G[:, m % 2], in_w[:, k, m * P:(m + 1) * P], xnT[:, par, k],
                                            start=(k == 0), stop=(k == KC - 1))
                last.then_inc(xz_mm.sem, 1)

        def front_xdbl(t, par):
            wait(pe, xz_evac, t, 2 * KD)
            for m in range(KD):
                wait(pe, xs_done, t, m + 1)
                last = nc.tensor.matmul(G[0:DT0 + R, 0], xp_w[:, m, :], xs[:, par, m], start=(m == 0), stop=(m == KD - 1))
            last.then_inc(xdbl_mm.sem, 1)

        def front_dt(t):
            wait(pe, dt_evac, t, 1)
            for m in range(KD):
                if m == 1:
                    wait(pe, bc_split, t, 1)
                    wait(pe, bc_step, t, 1)
                if m >= 2:
                    wait(pe, dtp_evac, t, m - 1)
                nc.tensor.matmul(G[:, (m + 1) % 2], dt_w[DT0:DT0 + R, m * P:(m + 1) * P], dtT[DT0:DT0 + R, :],
                                 start=True, stop=True).then_inc(dtp_mm.sem, 1)

        def back_out(t, par, last_one):
            wait(pe, yg_done, t, 1)
            wait(pe, x1_evac, t - 1, 2)
            if last_one:
                wait(pe, dtp_evac, t, KD)
            else:
                wait(pe, dtp_evac, t + 1, KD)
            for q in range(Q):
                o = G[:, q // 2, (q % 2) * C:(q % 2 + 1) * C]
                for m in range(KD):
                    last = nc.tensor.matmul(o, xs[:, par, m, q * P:(q + 1) * P], out_w[:, m, :],
                                            start=(m == 0), stop=(m == KD - 1))
                    for k in range(KC if m == 0 else 0):
                        nc.tensor.matmul(G[:, q // 2, (q % 2) * C + k * P:(q % 2) * C + (k + 1) * P],
                                         xnT[:, par, k, q * P:(q + 1) * P], skip_ident[:],
                                         start=False, stop=False, skip_group_check=True)
                last.then_inc(outp_mm.sem, 1)

        def back_T(t, after_front):
            wait(pe, ln2_norm, t, 1)
            if after_front:
                wait(pe, dtp_evac, t + 2, KD)
            for k in range(KC):
                for q in range(Q):
                    last = nc.tensor.transpose(G[:, k, q * P:(q + 1) * P], z2[:, q, k * P:(k + 1) * P], ident[:])
            last.then_inc(z2_T.sem, 1)

        def back_proj(t):
            wait(pe, z2_evac, t, 2)
            wait(pe, xr_loaded, t, 16)
            for k in range(KC):
                for c in range(KC):
                    last = nc.tensor.matmul(G[:, k], proj_w[:, c, bass.ds(k, P, KC)], z2T[:, c],
                                            start=(c == 0), stop=(c == KC - 1))
                    for q in range(Q if c == 0 else 0):
                        nc.tensor.matmul(G[:, k, q * P:(q + 1) * P], xr[:, q, bass.ds(k, P, KC)], ident[:],
                                         start=False, stop=False, skip_group_check=True)
                last.then_inc(x1_mm.sem, 1)

        def front(b, j, t, par, alone=False):
            front_T(t, True, False)
            front_xz(t, par, 0, 2 * KD)
            front_xdbl(t, par)
            front_dt(t)

        def period(b, j, t, par, has_back, has_front):
            f, fp = t + 1, 1 - par
            for n in range(N):
                spread(t, par, n)
                if n:
                    add_y(t, n - 1)
                if has_back and n == 0:
                    back_out(t - 1, 1 - par, False)
                if has_front:
                    if n == 3:
                        front_T(f, False, not has_back)
                    if n == 4:
                        front_xz(f, fp, 0, 3)
                    if n == 5:
                        front_xz(f, fp, 3, 6)
                    if n == 6:
                        front_xz(f, fp, 6, 8)
                    if n == 8:
                        front_xdbl(f, fp)
                    if n == 9:
                        front_dt(f)
                if has_back and n == 11:
                    back_T(t - 1, has_front)
                if has_back and n == 12:
                    back_proj(t - 1)
            add_y(t, N - 1)

        def back(b, j, t, par):
            back_out(t, par, True)
            back_T(t, False)
            back_proj(t)

        batch(pe, front, period, back)


K_STEPS, DT, BN_EPS, GN_EPS1 = 5, 0.2, 1e-3, 1e-5
ROWS = 4


def diffusion_layer(nc, a, ctx, ident, minus_half, x1_mv, B, H, W, C):
    KC = C // P
    NR = H // ROWS
    M = ROWS * W
    assert W == P and M == T and KC == 2 and NR % 2 == 0 and NR >= 6
    x1_dram = a["x1_dram"]
    x1_rows = x1_dram.rearrange("b k p (h w) -> b p k h w", w=W)
    out_tok = a["out"].rearrange("b h w c -> b (h w) c")

    def sb(name, shape, dt=F32):
        return ctx.enter_context(nc.sbuf_tensor(name, shape, dt))

    signals = []

    def signal(name, per):
        s = Signal(ctx.enter_context(nc.semaphore(name)), per)
        signals.append(s)
        return s

    def wait(eng, sig, t, k):
        eng.wait_ge(sig.sem, sig.of(t, k))

    avg4 = sb("avg4", [P, P])
    up_one = sb("up_one", [P, P])
    down_one = sb("down_one", [P, P])
    taps_w = sb("taps_w", [P, 2, 9, KC])
    taps = sb("taps", [P, 2, KC, 9, P])
    bn_in = sb("bn_in", [P, 3, 4, KC])
    bn_s = sb("bn_s", [P, 3, KC])
    bn_b = sb("bn_b", [P, 3, KC])
    g2_mean = sb("g2_mean", [P, B])
    g2_var = sb("g2_var", [P, B])
    g2_scale = sb("g2_scale", [P, B])
    g2_shift = sb("g2_shift", [P, B])
    g2_now = sb("g2_now", [P, 2])

    with (
        nc.psum_tensor("g2_psum", [P, 2, 512], F32) as g2_psum,
        nc.semaphore("c_loaded") as c_loaded,
        nc.semaphore("c_step") as c_step,
        nc.semaphore("c_mean") as c_mean,
        nc.semaphore("c_pow") as c_pow,
        nc.Block() as block,
    ):
        @block.sync
        def _(sp):
            for dst, src in ((avg4, "avg4"), (up_one, "up_one"), (down_one, "down_one"), (taps_w, "taps_w"), (bn_in, "bn_in")):
                sp.dma_start(dst[:], a[src]).then_inc(c_loaded, 16)

        @block.vector
        def _(dve):
            dve.wait_ge(c_loaded, 16 * 5)
            for c in range(2):
                for k in range(KC):
                    for i in range(9):
                        nc.vector.tensor_scalar(taps[:, c, k, i, :], ident[:], taps_w[:, c, i, k:k + 1], None, ALU.mult)
            nc.vector.tensor_scalar(bn_s[:], bn_in[:, :, 3, :], BN_EPS, None, ALU.add).then_inc(c_step, 1)
            dve.wait_ge(c_pow, 1)
            nc.vector.tensor_tensor(bn_s[:], bn_s[:], bn_in[:, :, 0, :], ALU.mult).then_inc(c_step, 1)
            dve.wait_ge(c_step, 2)
            nc.vector.tensor_tensor(bn_b[:], bn_in[:, :, 2, :], bn_s[:], ALU.mult).then_inc(c_step, 1)
            dve.wait_ge(c_step, 3)
            nc.vector.tensor_tensor(bn_b[:], bn_in[:, :, 1, :], bn_b[:], ALU.subtract).then_inc(c_step, 1)
            dve.wait_ge(c_step, 4)
            nc.vector.tensor_scalar(bn_s[:, 0:2, :], bn_s[:, 0:2, :], DT, None, ALU.mult)
            nc.vector.tensor_scalar(bn_b[:, 0:2, :], bn_b[:, 0:2, :], DT, None, ALU.mult)
            dve.wait_ge(c_mean, 1)
            nc.vector.tensor_copy(g2_mean[:], g2_psum[:, 0, 0:B]).then_inc(c_step, 1)
            dve.wait_ge(c_step, 5)
            nc.vector.tensor_tensor(g2_var[:], x1_mv[:, 0, :], g2_mean[:], ALU.subtract).then_inc(c_step, 1)
            dve.wait_ge(c_step, 6)
            nc.vector.tensor_tensor(g2_var[:], g2_var[:], g2_var[:], ALU.mult).then_inc(c_step, 1)
            dve.wait_ge(c_step, 7)
            nc.vector.tensor_tensor(g2_var[:], g2_var[:], x1_mv[:, 1, :], ALU.add).then_inc(c_step, 1)
            dve.wait_ge(c_mean, 2)
            nc.vector.tensor_scalar(g2_scale[:], g2_psum[:, 1, 0:B], GN_EPS1, None, ALU.add).then_inc(c_step, 1)
            dve.wait_ge(c_pow, 2)
            nc.vector.scalar_tensor_tensor(g2_shift[:], g2_mean[:], -1.0, g2_scale[:], ALU.mult, ALU.mult)

        @block.tensor
        def _(pe):
            pe.wait_ge(c_loaded, 16 * 5)
            nc.tensor.matmul(g2_psum[:, 0, 0:B], avg4[:], x1_mv[:, 0, :], start=True, stop=True).then_inc(c_mean, 1)
            pe.wait_ge(c_step, 8)
            nc.tensor.matmul(g2_psum[:, 1, 0:B], avg4[:], g2_var[:], start=True, stop=True).then_inc(c_mean, 1)

        @block.gpsimd
        def _(pool):
            half = minus_half[:, 0:3 * KC].rearrange("p (a k) -> p a k", k=KC)
            pool.wait_ge(c_step, 1)
            nc.gpsimd.tensor_tensor(bn_s[:], bn_s[:], half, ALU.pow).then_inc(c_pow, 1)
            pool.wait_ge(c_step, 9)
            nc.gpsimd.tensor_tensor(g2_scale[:], g2_scale[:], minus_half[:, 0:B], ALU.pow).then_inc(c_pow, 1)

    xh = sb("xh", [P, KC, ROWS + 2, W])
    sn = sb("sn", [P, KC, ROWS + 2, W + 2])
    hs = sb("hs", [P, 2, KC, ROWS, W + 2])
    ax = sb("ax", [P, KC, ROWS, W + 2])
    ay = sb("ay", [P, KC, ROWS, W])
    sum_w = sb("sum_w", [P, KC, ROWS + 2, W])
    dif_w = sb("dif_w", [P, KC, ROWS + 2, W])
    gy = sb("gy2", [P, KC, ROWS, W])
    gx = sb("gx2", [P, KC, ROWS, W])
    pq = sb("pq", [P, KC, ROWS, W])
    den = sb("den", [P, KC, ROWS, W])
    dd = sb("dd", [P, KC, ROWS, W])
    dbx = sb("dbx", [P, KC, ROWS, W])
    dby = sb("dby", [P, KC, ROWS, W])
    c_old = sb("c_old", [P, 2, KC, ROWS, W])
    c_own = sb("c_own", [P, 2, KC, ROWS, W])
    c_left = sb("c_left", [P, 2, KC, ROWS, W])
    c_right = sb("c_right", [P, 2, KC, ROWS, W])
    c_moved = sb("c_moved", [P, 2, KC, ROWS, W])
    c_same = sb("c_same", [P, 2, KC, ROWS, W])
    src = sb("src", [P, 2, KC, ROWS, W])
    src1 = sb("src1", [P, KC, ROWS, W])
    src2 = sb("src2", [P, KC, ROWS, W])
    hb = sb("hb", [P, 3, KC, ROWS, W + 2])
    q_old = sb("q_old", [P, KC, ROWS, W])
    q_own = sb("q_own", [P, KC, ROWS, W])
    q_left = sb("q_left", [P, KC, ROWS, W])
    q_right = sb("q_right", [P, KC, ROWS, W])
    q_moved = sb("q_moved", [P, KC, ROWS, W])
    q_same = sb("q_same", [P, KC, ROWS, W])
    xres = sb("xres", [P, KC, ROWS, W])
    fo = sb("fo", [P, KC, ROWS, W])
    ot = sb("ot", [P, ROWS, C])

    acc_ps = ctx.enter_context(nc.psum_tensor("acc_ps", [P, KC, ROWS, W], F32))
    moved_ps = ctx.enter_context(nc.psum_tensor("moved_ps", [P, KC, ROWS, W], F32))
    conv_ps = ctx.enter_context(nc.psum_tensor("conv_ps", [P, 2 * KC, ROWS, W], F32))

    xh_loaded = signal("xh_loaded", 32)
    sn_done = signal("sn_done", 1)
    hs_done = signal("hs_done", 1)
    conv_mm = signal("conv_mm", 2 * KC)
    ax_done = signal("ax_done", 1)
    ay_done = signal("ay_done", 1)
    ay_moved = signal("ay_moved", 1)
    ay_used = signal("ay_used", 1)
    sums_done = signal("sums_done", 2)
    sob = signal("sob", 4)
    squared = signal("squared", 1)
    coef = signal("coef", 9)
    da_done = signal("da_done", 3)
    e2_done = signal("e2_done", 4)
    src_done = signal("src_done", 1)
    dv_done = signal("dv_done", 2)
    old_done = signal("old_done", 2)
    src_steps = signal("src_steps", 4)
    q_old_done = signal("q_old_done", 2 * (K_STEPS - 2))
    q_own_done = signal("q_own_done", K_STEPS - 1)
    q_left_done = signal("q_left_done", K_STEPS)
    q_right_done = signal("q_right_done", K_STEPS)
    q_same_done = signal("q_same_done", K_STEPS)
    q_moved_done = signal("q_moved_done", 2 * K_STEPS)
    moved = signal("moved", K_STEPS)
    acc_done = signal("acc_done", K_STEPS)
    h_done = signal("h_done", K_STEPS)
    wrapped = signal("wrapped", K_STEPS)
    xres_loaded = signal("xres_loaded", 16)
    fo_done = signal("fo_done", 1)
    added = signal("added", 1)
    fo_T = signal("fo_T", 1)
    ot_done = signal("ot_done", 1)
    out_stored = signal("out_stored", 16)

    def state(par, it):
        return hs[:, par] if it == 0 else hb[:, (it - 1) % 3]

    batch_norm = ctx.enter_context(nc.semaphore("batch_norm"))

    def flat(t):
        return t.rearrange("p k r w -> p k (r w)")

    block = ctx.enter_context(nc.Block())

    def batch(eng, prep, period, finish):
        with eng.Fori(0, B) as b:
            u0 = b * NR
            prep(b, 0, u0, 0, top=True)
            period(b, 0, u0, 0, finishes=False, prepares=True)
            with eng.Fori(0, NR // 2 - 2) as i:
                period(b, i * 2 + 1, u0 + i * 2 + 1, 1, finishes=True, prepares=True)
                period(b, i * 2 + 2, u0 + i * 2 + 2, 0, finishes=True, prepares=True)
            period(b, NR - 3, u0 + NR - 3, 1, finishes=True, prepares=True)
            period(b, NR - 2, u0 + NR - 2, 0, finishes=True, prepares=True, bottom=True)
            period(b, NR - 1, u0 + NR - 1, 1, finishes=True, prepares=False)
            finish(b, NR - 1, u0 + NR - 1)

    @block.sync
    def _(sp):
        for s in signals:
            sp.sem_inc(s.sem, LEAD * s.per)

        def prep(b, r, u, par, top=False, bottom=False):
            wait(sp, hs_done, u - 1, 1)
            if top:
                sp.dma_start(xh[:, :, 1:], x1_rows[b, :, :, 0:ROWS + 1, :]).then_inc(xh_loaded.sem, 16)
                sp.dma_start(xh[:, :, 0:1], x1_rows[b, :, :, 1:2, :]).then_inc(xh_loaded.sem, 16)
            elif bottom:
                sp.dma_start(xh[:, :, 0:ROWS + 1], x1_rows[b, :, :, H - ROWS - 1:H, :]).then_inc(xh_loaded.sem, 16)
                sp.dma_start(xh[:, :, ROWS + 1:], x1_rows[b, :, :, H - 2:H - 1, :]).then_inc(xh_loaded.sem, 16)
            else:
                for k in range(KC):
                    sp.dma_start(xh[:, k], x1_rows[b, :, k, bass.ds(r * ROWS - 1, ROWS + 2), :]
                                 ).then_inc(xh_loaded.sem, 16)

        def load_residual(b, r, u):
            wait(sp, added, u - 1, 1)
            sp.dma_start(xres[:], x1_rows[b, :, :, bass.ds(r * ROWS, ROWS), :]).then_inc(xres_loaded.sem, 16)

        def finish(b, r, u):
            load_residual(b, r, u)
            wait(sp, ot_done, u, 1)
            sp.dma_start(out_tok[b, bass.ds(r * M, M), :].rearrange("(q p) c -> p q c", p=P), ot[:]
                         ).then_inc(out_stored.sem, 16)

        def period(b, r, u, par, finishes, prepares, bottom=False):
            if prepares:
                prep(b, r + 1, u + 1, 1 - par, bottom=bottom)
            if finishes:
                finish(b, r - 1, u - 1)

        batch(sp, prep, period, finish)
        wait(sp, out_stored, B * NR - 1, 16)

    @block.scalar
    def _(act):
        def norm(b, u, par):
            scale, bias = g2_now[:, 0:1], g2_now[:, 1:2]

            def put(dst, columns):
                return nc.scalar.activation(dst, columns, ACT.Identity, bias=bias, scale=scale)

            wait(act, xh_loaded, u, 32)
            wait(act, conv_mm, u - 1, 2 * KC)
            wait(act, sums_done, u - 1, 2)
            wait(act, sob, u - 1, 1)
            put(sn[:, :, :, 1:W + 1].rearrange("p k r w -> p (k r) w"), xh[:].rearrange("p k r w -> p (k r) w"))
            put(sn[:, :, :, 0], xh[:, :, :, 1])
            put(sn[:, :, :, W + 1], xh[:, :, :, W - 2]).then_inc(sn_done.sem, 1)
            inner = xh[:, :, 1:ROWS + 1, :]
            put(hs[:, par, :, :, 1:W + 1], inner)
            put(hs[:, par, :, :, 0], inner[:, :, :, W - 1])
            put(hs[:, par, :, :, W + 1], inner[:, :, :, 0]).then_inc(hs_done.sem, 1)

        def squares(u):
            wait(act, sob, u, 4)
            nc.scalar.activation(flat(gy[:]), flat(gy[:]), ACT.Square, scale=0.5)
            nc.scalar.activation(flat(gx[:]), flat(gx[:]), ACT.Square, scale=0.5).then_inc(squared.sem, 1)

        def fluxes(u, conv):
            if conv == 0:
                wait(act, e2_done, u - 1, 1)
                wait(act, da_done, u - 1, 1)
            else:
                wait(act, dv_done, u - 1, 1)
                wait(act, ay_used, u - 1, 1)
            for k in range(KC):
                scale, bias = bn_s[:, conv, k:k + 1], bn_b[:, conv, k:k + 1]
                ps = conv_ps[:, conv * KC + k]
                wait(act, conv_mm, u, conv * KC + k + 1)
                if conv == 0:
                    nc.scalar.activation(ax[:, k, :, 1:W + 1], ps, ACT.Relu, bias=bias, scale=scale)
                    nc.scalar.activation(ax[:, k, :, 0], ps[:, :, W - 1], ACT.Relu, bias=bias, scale=scale)
                    last = nc.scalar.activation(ax[:, k, :, W + 1], ps[:, :, 0], ACT.Relu, bias=bias, scale=scale)
                else:
                    last = nc.scalar.activation(ay[:, k], ps, ACT.Relu, bias=bias, scale=scale)
            last.then_inc((ay_done if conv else ax_done).sem, 1)

        def finish_relu(u):
            wait(act, h_done, u, K_STEPS)
            wait(act, fo_T, u - 1, 1)
            for k in range(KC):
                last = nc.scalar.activation(fo[:, k], hb[:, (K_STEPS - 1) % 3, k, :, 1:W + 1], ACT.Relu,
                                            bias=bn_b[:, 2, k:k + 1], scale=bn_s[:, 2, k:k + 1])
            last.then_inc(fo_done.sem, 1)

        def finish_out(u):
            wait(act, fo_T, u, 1)
            wait(act, out_stored, u - 1, 16)
            for k in range(KC):
                last = nc.scalar.copy(ot[:, :, bass.ds(k, P, KC)], conv_ps[:, KC + k])
            last.then_inc(ot_done.sem, 1)

        def prep(b, r, u, par, top=False, bottom=False):
            nc.scalar.copy(g2_now[:, 0:1], g2_scale[:, bass.ds(b, 1)])
            nc.scalar.copy(g2_now[:, 1:2], g2_shift[:, bass.ds(b, 1)]).then_inc(batch_norm, 1)
            act.wait_ge(batch_norm, b + 1)
            norm(b, u, par)
            squares(u)
            fluxes(u, 0)
            fluxes(u, 1)

        def finish(b, r, u):
            finish_relu(u)
            finish_out(u)

        def period(b, r, u, par, finishes, prepares, bottom=False):
            if finishes:
                finish_relu(u - 1)
            if prepares:
                norm(b, u + 1, 1 - par)
            if finishes:
                finish_out(u - 1)
            if prepares:
                squares(u + 1)
                fluxes(u + 1, 0)
                fluxes(u + 1, 1)

        batch(act, prep, period, finish)

    @block.gpsimd
    def _(pool):
        tt = nc.gpsimd.tensor_tensor

        def sums(u):
            wait(pool, sn_done, u, 1)
            wait(pool, sob, u - 1, 4)
            rows = "p k r w -> p (k r) w"
            left, right = sn[:, :, :, 0:W].rearrange(rows), sn[:, :, :, 2:W + 2].rearrange(rows)
            tt(sum_w[:].rearrange(rows), left, right, ALU.add).then_inc(sums_done.sem, 1)
            tt(dif_w[:].rearrange(rows), right, left, ALU.subtract).then_inc(sums_done.sem, 1)

        def old_factor(u, par):
            wait(pool, coef, u, 9)
            tt(flat(c_old[:, par]), flat(dd[:]), flat(dbx[:]), ALU.subtract).then_inc(old_done.sem, 1)
            wait(pool, old_done, u, 1)
            tt(flat(c_old[:, par]), flat(c_old[:, par]), flat(dby[:]), ALU.subtract).then_inc(old_done.sem, 1)

        def channel_factors(u, par):
            wait(pool, ay_done, u, 1)
            dv = src2
            wait(pool, coef, u, 9)
            wait(pool, acc_done, u - 1, 2)
            tt(flat(dv[:]), flat(dd[:]), flat(ay[:]), ALU.mult).then_inc(dv_done.sem, 1)
            wait(pool, dv_done, u, 1)
            tt(c_moved[:, par, 0], dby[:, 0], dv[:, 0], ALU.subtract)
            tt(c_moved[:, par, 1], dby[:, 1], dv[:, 1], ALU.add)
            tt(c_same[:, par, 0], dby[:, 0], dv[:, 0], ALU.add)
            tt(c_same[:, par, 1], dby[:, 1], dv[:, 1], ALU.subtract).then_inc(dv_done.sem, 1)

        def sources(u, par):
            wait(pool, src_done, u, 1)
            wait(pool, old_done, u, 2)
            wait(pool, dv_done, u, 2)
            fsrc = hs[:, par, :, :, 1:W + 1]
            tt(src2[:], c_old[:, par], fsrc, ALU.mult).then_inc(src_steps.sem, 1)
            wait(pool, e2_done, u, 4)
            wait(pool, acc_done, u - 1, 1)
            tt(src1[:], c_own[:, par], fsrc, ALU.mult).then_inc(src_steps.sem, 1)
            wait(pool, src_steps, u, 2)
            tt(flat(src2[:]), flat(src2[:]), flat(src[:, par]), ALU.add).then_inc(src_steps.sem, 1)
            wait(pool, src_steps, u, 3)
            tt(flat(src1[:]), flat(src1[:]), flat(src2[:]), ALU.add).then_inc(src_steps.sem, 1)

        def old_term(u, par, it):
            if it == 2:
                wait(pool, h_done, u, 1)
                wait(pool, acc_done, u - 1, K_STEPS)
            else:
                wait(pool, acc_done, u, it)
                wait(pool, h_done, u, it - 1)
            tt(q_old[:], c_old[:, par], state(par, it - 1)[:, :, :, 1:W + 1], ALU.mult).then_inc(q_old_done.sem, 1)
            wait(pool, q_old_done, u, 2 * (it - 2) + 1)
            tt(flat(q_old[:]), flat(q_old[:]), flat(src[:, par]), ALU.add).then_inc(q_old_done.sem, 1)

        def add_residual(u):
            wait(pool, fo_done, u, 1)
            wait(pool, xres_loaded, u, 16)
            tt(flat(fo[:]), flat(fo[:]), flat(xres[:]), ALU.add).then_inc(added.sem, 1)

        def prep(b, r, u, par, top=False, bottom=False):
            sums(u)
            old_factor(u, par)
            channel_factors(u, par)
            sources(u, par)

        def finish(b, r, u):
            add_residual(u)

        def period(b, r, u, par, finishes, prepares, bottom=False):
            if finishes:
                add_residual(u - 1)
            if prepares:
                sums(u + 1)
            old_term(u, par, 2)
            if prepares:
                old_factor(u + 1, 1 - par)
            old_term(u, par, 3)
            if prepares:
                channel_factors(u + 1, 1 - par)
            old_term(u, par, 4)
            if prepares:
                sources(u + 1, 1 - par)

        batch(pool, prep, period, finish)

    @block.vector
    def _(dve):
        tt, stt, ts = nc.vector.tensor_tensor, nc.vector.scalar_tensor_tensor, nc.vector.tensor_scalar

        def step(u, par, it):
            h = state(par, it)
            if it == 0:
                wait(dve, hs_done, u, 1)
                wait(dve, da_done, u, 3)
                wait(dve, dv_done, u, 2)
            else:
                wait(dve, wrapped, u, it)
                wait(dve, h_done, u, it)
                if it == 1:
                    wait(dve, e2_done, u, 4)
            tt(q_left[:], c_left[:, par], h[:, :, :, 0:W], ALU.mult).then_inc(q_left_done.sem, 1)
            tt(q_right[:], c_right[:, par], h[:, :, :, 2:W + 2], ALU.mult).then_inc(q_right_done.sem, 1)
            if it:
                tt(q_own[:], c_own[:, par], h[:, :, :, 1:W + 1], ALU.mult).then_inc(q_own_done.sem, 1)
            for k in range(KC):
                last = tt(q_same[:, k], c_same[:, par, k], h[:, 1 - k, :, 1:W + 1], ALU.mult)
            last.then_inc(q_same_done.sem, 1)
            wait(dve, moved, u, it + 1)
            tt(flat(q_moved[:]), flat(c_moved[:, par]), flat(moved_ps[:]), ALU.mult).then_inc(q_moved_done.sem, 1)
            wait(dve, q_moved_done, u, 2 * it + 1)
            wait(dve, q_same_done, u, it + 1)
            tt(flat(q_moved[:]), flat(q_moved[:]), flat(q_same[:]), ALU.add).then_inc(q_moved_done.sem, 1)
            wait(dve, q_moved_done, u, 2 * it + 2)
            wait(dve, acc_done, u, it + 1)
            if it == 1:
                wait(dve, fo_done, u - 1, 1)
            if it == 3:
                wait(dve, q_old_done, u, 2)
            if it == 4:
                wait(dve, q_old_done, u, 4)
            new = hb[:, it % 3]
            tt(new[:, :, :, 1:W + 1], acc_ps[:], q_moved[:], ALU.add).then_inc(h_done.sem, 1)
            wait(dve, h_done, u, it + 1)
            if it < K_STEPS - 1:
                nc.vector.tensor_copy(new[:, :, :, 0], new[:, :, :, W])
                nc.vector.tensor_copy(new[:, :, :, W + 1], new[:, :, :, 1]).then_inc(wrapped.sem, 1)
            else:
                nc.vector.tensor_copy(new[:, :, :, W + 1], new[:, :, :, 1]).then_inc(wrapped.sem, 1)

        def sobel(u):
            wait(dve, sums_done, u, 2)
            wait(dve, sn_done, u, 1)
            wait(dve, coef, u - 1, 9)
            rows = "p k r w -> p (k r) w"
            stt(sum_w[:].rearrange(rows), sn[:, :, :, 1:W + 1].rearrange(rows), 2.0, sum_w[:].rearrange(rows),
                ALU.mult, ALU.add).then_inc(sob.sem, 1)
            tt(flat(gx[:]), flat(dif_w[:, :, 0:ROWS]), flat(dif_w[:, :, 2:ROWS + 2]), ALU.add).then_inc(sob.sem, 1)
            wait(dve, sob, u, 1)
            tt(flat(gy[:]), flat(sum_w[:, :, 2:ROWS + 2]), flat(sum_w[:, :, 0:ROWS]), ALU.subtract).then_inc(sob.sem, 1)
            wait(dve, sob, u, 2)
            stt(flat(gx[:]), flat(dif_w[:, :, 1:ROWS + 1]), 2.0, flat(gx[:]), ALU.mult, ALU.add).then_inc(sob.sem, 1)

        def diffusivities(u):
            wait(dve, squared, u, 1)
            ts(gy[:], gy[:], 1.0, None, ALU.add).then_inc(coef.sem, 1)
            ts(gx[:], gx[:], 1.0, None, ALU.add).then_inc(coef.sem, 1)
            wait(dve, coef, u, 2)
            tt(flat(pq[:]), flat(gy[:]), flat(gx[:]), ALU.mult).then_inc(coef.sem, 1)
            tt(flat(den[:]), flat(gy[:]), flat(gx[:]), ALU.add).then_inc(coef.sem, 1)
            wait(dve, coef, u, 4)
            stt(flat(den[:]), flat(den[:]), 2 * DT, flat(pq[:]), ALU.mult, ALU.add).then_inc(coef.sem, 1)
            wait(dve, coef, u, 5)
            nc.vector.reciprocal(flat(den[:]), flat(den[:])).then_inc(coef.sem, 1)
            wait(dve, coef, u, 6)
            wait(dve, dv_done, u - 1, 2)
            wait(dve, old_done, u - 1, 2)
            tt(flat(dd[:]), flat(pq[:]), flat(den[:]), ALU.mult).then_inc(coef.sem, 1)
            stt(flat(dbx[:]), flat(gx[:]), 2 * DT, flat(den[:]), ALU.mult, ALU.mult).then_inc(coef.sem, 1)
            stt(flat(dby[:]), flat(gy[:]), 2 * DT, flat(den[:]), ALU.mult, ALU.mult).then_inc(coef.sem, 1)

        def row_factors(u, par):
            wait(dve, coef, u, 9)
            wait(dve, ax_done, u, 1)
            da = c_own[:, par]
            tt(da, dd[:], ax[:, :, :, 1:W + 1], ALU.mult).then_inc(da_done.sem, 1)
            wait(dve, da_done, u, 1)
            tt(flat(c_left[:, par]), flat(dbx[:]), flat(da), ALU.subtract).then_inc(da_done.sem, 1)
            tt(flat(c_right[:, par]), flat(dbx[:]), flat(da), ALU.add).then_inc(da_done.sem, 1)

        def own_factor(u, par):
            wait(dve, coef, u, 9)
            e2, e2y = den, pq
            wait(dve, ax_done, u, 1)
            tt(e2[:], ax[:, :, :, 0:W], ax[:, :, :, 2:W + 2], ALU.subtract).then_inc(e2_done.sem, 1)
            stt(src[:, par], dd[:], 2 * DT, hs[:, par, :, :, 1:W + 1], ALU.mult, ALU.mult).then_inc(src_done.sem, 1)
            wait(dve, ay_moved, u, 1)
            wait(dve, ay_done, u, 1)
            tt(e2y[:, 0], conv_ps[:, 0], ay[:, 1], ALU.subtract)
            tt(e2y[:, 1], ay[:, 0], conv_ps[:, 1], ALU.subtract).then_inc(ay_used.sem, 1)
            wait(dve, ay_used, u, 1)
            wait(dve, e2_done, u, 1)
            tt(flat(e2[:]), flat(e2[:]), flat(e2y[:]), ALU.add).then_inc(e2_done.sem, 1)
            wait(dve, e2_done, u, 2)
            wait(dve, da_done, u, 3)
            stt(flat(c_own[:, par]), flat(dd[:]), -1.0, flat(e2[:]), ALU.mult, ALU.mult).then_inc(e2_done.sem, 2)

        def prep(b, r, u, par, top=False, bottom=False):
            sobel(u)
            diffusivities(u)
            row_factors(u, par)
            own_factor(u, par)

        def finish(b, r, u):
            pass

        def period(b, r, u, par, finishes, prepares, bottom=False):
            for it in range(K_STEPS):
                step(u, par, it)
                if prepares:
                    if it == 0:
                        sobel(u + 1)
                    if it == 1:
                        diffusivities(u + 1)
                    if it == 2:
                        row_factors(u + 1, 1 - par)
                    if it == 3:
                        own_factor(u + 1, 1 - par)

        batch(dve, prep, period, finish)

    @block.tensor
    def _(pe):
        def step(u, par, it):
            h = state(par, it)
            if it == 0:
                wait(pe, hs_done, u, 1)
                wait(pe, h_done, u - 1, K_STEPS)
            else:
                wait(pe, h_done, u, it)
            nc.tensor.matmul(moved_ps[:, 0], down_one[:], h[:, 1, :, 1:W + 1], start=True, stop=True)
            nc.tensor.matmul(moved_ps[:, 1], up_one[:], h[:, 0, :, 1:W + 1], start=True, stop=True
                             ).then_inc(moved.sem, 1)
            if it == 0:
                wait(pe, src_steps, u, 4)
                terms = [src1[:]]
            elif it == 1:
                terms = [src2[:]]
            else:
                wait(pe, q_old_done, u, 2 * (it - 2) + 2)
                terms = [q_old]
            terms += [q_left, q_right] + ([q_own] if it else [])
            for i, term in enumerate(terms):
                if i == 1:
                    wait(pe, q_left_done, u, it + 1)
                if i == 2:
                    wait(pe, q_right_done, u, it + 1)
                if i == 3:
                    wait(pe, q_own_done, u, it)
                for k in range(KC):
                    last = nc.tensor.matmul(acc_ps[:, k], ident[:], term[:, k], start=(i == 0), stop=(i == len(terms) - 1))
            last.then_inc(acc_done.sem, 1)

        def convolve(u, conv, top, bottom):
            if conv == 0:
                wait(pe, sn_done, u, 1)
                wait(pe, ay_used, u - 1, 1)
            else:
                wait(pe, ot_done, u - 2, 1)
            last_full = 0 if bottom else 2
            order = [(1, 1)] + [(i, j) for i in range(3) for j in range(3)
                                if (i, j) not in ((1, 1), (last_full, 1))] + [(last_full, 1)]
            for k in range(KC):
                for n, (i, j) in enumerate(order):
                    r0 = 1 if top and i == 0 else 0
                    r1 = ROWS - 1 if bottom and i == 2 else ROWS
                    w0, w1 = max(0, 1 - j), min(W, W + 1 - j)
                    last = nc.tensor.matmul(conv_ps[:, conv * KC + k, r0:r1, w0:w1], taps[:, conv, k, 3 * i + j, :],
                                            sn[:, k, r0 + i:r1 + i, w0 + j:w1 + j],
                                            start=(n == 0), stop=(n == 8), skip_group_check=(0 < n < 8))
                last.then_inc(conv_mm.sem, 1)

        def move_ay(u):
            wait(pe, ay_done, u, 1)
            wait(pe, ax_done, u, 1)
            nc.tensor.matmul(conv_ps[:, 0], down_one[:], ay[:, 1], start=True, stop=True)
            nc.tensor.matmul(conv_ps[:, 1], up_one[:], ay[:, 0], start=True, stop=True).then_inc(ay_moved.sem, 1)

        def finish_T(u, after_prep):
            wait(pe, added, u, 1)
            wait(pe, ay_done, u + after_prep, 1)
            for k in range(KC):
                for r in range(ROWS):
                    last = nc.tensor.transpose(conv_ps[:, KC + k, r, :], fo[:, k, r, :], ident[:])
            last.then_inc(fo_T.sem, 1)

        def prep(b, r, u, par, top=False, bottom=False):
            wait(pe, ot_done, u - 1, 1)
            convolve(u, 0, top, bottom)
            convolve(u, 1, top, bottom)
            move_ay(u)

        def finish(b, r, u):
            finish_T(u, 0)

        def period(b, r, u, par, finishes, prepares, bottom=False):
            for it in range(K_STEPS):
                step(u, par, it)
                if it == 0:
                    if finishes:
                        finish_T(u - 1, 1)
                    if prepares:
                        convolve(u + 1, 0, False, bottom)
                if it == 1 and prepares:
                    convolve(u + 1, 1, False, bottom)
                if it == 2 and prepares:
                    move_ay(u + 1)

        batch(pe, prep, period, finish)


def constants():
    N = 16
    ident = np.eye(P, dtype=np.float32)
    avg_all = np.full((P, P), 1.0 / P, np.float32)
    select = np.zeros((6 * N, 2 * N, P), np.uint16)
    for part in range(3):
        for n in range(2 * N):
            select[2 * N * part + n, n, :] = 0x3F80
    avg4 = np.kron(np.eye(P // 4, dtype=np.float32), np.full((4, 4), 0.25, np.float32))
    down_one = np.roll(ident, 1, axis=1)
    up_one = np.roll(ident, -1, axis=1)
    return {"avg4": avg4, "down_one": down_one, "up_one": up_one, "ident": ident, "avg_all": avg_all, "select": select}


def arrays_of(inputs):
    L0 = {k[len("L0_conv_"):]: np.asarray(v) for k, v in inputs.items() if k.startswith("L0_conv_")}
    r = {"x": np.asarray(inputs["x"])}
    for k in ("in_proj_w", "x_proj_w", "dt_proj_w", "out_proj_w", "proj_w"):
        r[k + "T"] = np.ascontiguousarray(L0.pop(k).T)
    for k in ("conv_b", "dt_proj_b", "D", "ln_g", "ln_b"):
        L0[k] = L0[k].reshape(-1, P).T
    L0["proj_b"] = L0["proj_b"].reshape(P, -1)
    r.update(L0)
    L1 = {k[len("L1_conv_"):]: np.asarray(v) for k, v in inputs.items() if k.startswith("L1_conv_")}
    r["taps_w"] = np.stack([L1[k].reshape(9, P, 2).transpose(1, 0, 2) for k in ("wg", "wg1")], axis=1)
    r["bn_in"] = np.stack([np.stack([L1[f"{g}_{v}"].reshape(P, 2) for v in ("gamma", "beta", "mean", "var")], axis=1)
                           for g in ("g", "g1", "out")], axis=1)
    r.update(constants())
    return {k: np.ascontiguousarray(v) for k, v in r.items()}


def kernel(**inputs):
    import concourse.bacc as bacc
    from concourse.bass_utils import run_bass_kernel_spmd

    nc = bacc.Bacc("TRN2", target_bir_lowering=False, num_devices=1)
    given = arrays_of(inputs)
    arrays = {f"in_{k}": v for k, v in given.items()}
    a = {k: nc.dram_tensor(f"in_{k}", list(v.shape), mybir.dt.from_np(v.dtype), kind="ExternalInput").ap()
         for k, v in given.items()}
    B, H, W, C = given["x"].shape
    a["x1_dram"] = nc.dram_tensor("x1_dram", [B, C // P, P, H * W], F32, kind="Internal").ap()
    a["out"] = nc.dram_tensor("out_0", [B, H, W, C], F32, kind="ExternalOutput").ap()
    token_mixer(nc, a)
    return run_bass_kernel_spmd(nc, [arrays], core_ids=[0]).results[0]["out_0"]
```

```python
import numpy as np
import concourse.bass as bass
from concourse import mybir
from contextlib import ExitStack

F32 = mybir.dt.float32
BF16 = mybir.dt.bfloat16
U8 = mybir.dt.uint8
ALU = mybir.AluOpType
ACT = mybir.ActivationFunctionType

P = 128
T = 512
LEAD = 2
GN_EPS0, LN_EPS = 1e-5, 1e-5
GROUPS = 32
SIDE_SUMS = (0, 1, 2, 3, 4)
POOL_SUMS = (1, 2, 3)
CONV_PIECES = (0, 6, 14, 25, 36)
POOL_STEPS = (1, 3, 5, 7, 9, 11, 13)
STATE_BUFFER = (0, 1, 2, 0, 1, 2, 0, 1, 2, 0, 1, 2, 0, 1, 2, 1)
SERIES_BELOW = 2.0 ** -6


class Signal:

    def __init__(self, sem, per):
        self.sem, self.per = sem, per

    def of(self, t, k):
        return t * self.per + (LEAD * self.per + k)


def token_mixer(nc, a, debug=False):
    x = a["x"]
    B, H, W, C = x.shape
    L = H * W
    NCH = L // T
    Q = T // P
    KC = C // P
    DI = a["in_proj_wT"].shape[1] // 2
    KD = DI // P
    N = a["A_log"].shape[1]
    R = a["dt_proj_wT"].shape[0]
    DT0 = 3 * 2 * N
    TAPS = a["conv_w"].shape[1]
    HALO = TAPS - 1
    CG = C // GROUPS
    assert T % P == 0 and KC == 2 and KD == 4 and N == 16 and NCH >= 4 and NCH % 2 == 0

    x_tok = x.rearrange("b h w c -> b (h w) c")
    ctx = ExitStack()
    with ctx:
        def sb(name, shape, dt=F32):
            return ctx.enter_context(nc.sbuf_tensor(name, shape, dt))

        def signal(name, per):
            s = Signal(ctx.enter_context(nc.semaphore(name)), per)
            signals.append(s)
            return s

        def sem(name):
            return ctx.enter_context(nc.semaphore(name))

        signals = []
        x1_dram = a["x1_dram"]

        ident = sb("ident", [P, P])
        minus_half = sb("minus_half", [P, GROUPS])
        x1_mv = sb("x1_mv", [P, 2, B])
        all_layers, ctx = ctx, ExitStack()
        avg_all = sb("avg_all", [P, P])
        select = sb("select", [DT0, 2 * N, P], BF16)
        in_w = sb("in_w", [P, KC, 2 * DI])
        xp_w = sb("xp_w", [P, KD, DT0 + R])
        dt_w = sb("dt_w", [P, DI])
        out_w = sb("out_w", [P, KD, C])
        proj_w = sb("proj_w", [P, KC, C])
        conv_w = sb("conv_w", [P, KD, TAPS])
        conv_b = sb("conv_b", [P, KD])
        dt_b = sb("dt_b", [P, KD])
        skip_D = sb("skip_D", [P, KD])
        a_log = sb("a_log", [P, KD, N])
        decay = sb("decay", [P, KD, N])
        ln_g = sb("ln_g", [P, KC])
        ln_b = sb("ln_b", [P, KC])
        proj_b = sb("proj_b", [P, KC])
        skip_s = sb("skip_s", [P, 1])
        skip_ident = sb("skip_ident", [P, P])
        zeros = sb("zeros", [P, KD * N])
        gn_scale = sb("gn_scale", [P, B, GROUPS])
        gn_shift = sb("gn_shift", [P, B, GROUPS])

        loaded = sem("weights_loaded")
        loads = [(ident[:], a["ident"]), (avg_all[:], a["avg_all"]), (select[:].bitcast(mybir.dt.uint16), a["select"]),
                 (in_w[:], a["in_proj_wT"].rearrange("(k p) m -> p k m", p=P)),
                 (dt_w[DT0:DT0 + R, :], a["dt_proj_wT"]),
                 (out_w[:], a["out_proj_wT"].rearrange("(k p) m -> p k m", p=P)),
                 (proj_w[:], a["proj_wT"].rearrange("(k p) m -> p k m", p=P)),
                 (conv_w[:], a["conv_w"].rearrange("(k p) m -> p k m", p=P)),
                 (a_log[:], a["A_log"].rearrange("(k p) m -> p k m", p=P)),
                 (conv_b[:], a["conv_b"]),
                 (dt_b[:], a["dt_proj_b"]),
                 (skip_D[:], a["D"]),
                 (ln_g[:], a["ln_g"]),
                 (ln_b[:], a["ln_b"]),
                 (proj_b[:], a["proj_b"]),
                 (skip_s[:], a["skip_scale"].partition_broadcast(P))]
        xp_T = a["x_proj_wT"].rearrange("(k p) m -> p k m", p=P)
        loads += [(xp_w[:, :, 2 * N * i:2 * N * (i + 1)], xp_T[:, :, R:R + 2 * N]) for i in range(3)]
        loads += [(xp_w[:, :, DT0:DT0 + R], xp_T[:, :, 0:R])]

        SQ = 16
        while (L // (P * SQ)) < 1 or L % (P * SQ):
            SQ //= 2
        NT = L // (P * SQ)
        x_stat = x.rearrange("b h w c -> (b h w) c").rearrange("(n p q) c -> n p q c", p=P, q=SQ)
        with (
            nc.sbuf_tensor("stat_x", [P, 2, SQ, C], F32) as stat_x,
            nc.sbuf_tensor("stat_bn", [P, GROUPS, NT, 6], F32) as stat_bn,
            nc.sbuf_tensor("stat_mv", [P, 2, GROUPS], F32) as stat_mv,
            nc.sbuf_tensor("stat_diff", [P, GROUPS], F32) as stat_diff,
            nc.sbuf_tensor("stat_mean", [P, GROUPS], F32) as stat_mean,
            nc.sbuf_tensor("stat_rstd", [P, GROUPS], F32) as stat_rstd,
            nc.psum_tensor("stat_psum", [P, 2, 512], F32) as stat_psum,
            nc.semaphore("stat_loaded0") as stat_loaded0,
            nc.semaphore("stat_loaded1") as stat_loaded1,
            nc.semaphore("stat_tile_done") as stat_tile_done,
            nc.semaphore("stat_step") as stat_step,
            nc.semaphore("stat_averaged") as stat_averaged,
            nc.semaphore("stat_pow") as stat_pow,
            nc.semaphore("const_ready") as const_ready,
            nc.semaphore("act_ready") as act_ready,
            nc.Block() as block,
        ):
            stat_loaded = [stat_loaded0, stat_loaded1]
            steps_per_batch = 7

            @block.sync
            def _(sp):
                for dst, src in loads:
                    sp.dma_start(dst, src).then_inc(loaded, 16)
                for b in range(B):
                    for n in range(NT):
                        i = b * NT + n
                        if i >= 2:
                            sp.wait_ge(stat_tile_done, i - 1)
                        sp.dma_start(stat_x[:, i % 2], x_stat[i]).then_inc(stat_loaded[i % 2], 16)

            @block.vector
            def _(dve):
                nc.vector.memset(zeros[:], 0.0)
                nc.vector.memset(minus_half[:], -0.5).then_inc(const_ready, 1)
                for b in range(B):
                    for n in range(NT):
                        i = b * NT + n
                        dve.wait_ge(stat_loaded[i % 2], 16 * (i // 2 + 1))
                        for g in range(GROUPS):
                            last = nc.vector.bn_stats(stat_bn[:, g, n, :], stat_x[:, i % 2, :, g * CG:(g + 1) * CG])
                        last.then_inc(stat_tile_done, 1)
                    done = b * steps_per_batch
                    dve.wait_ge(stat_tile_done, (b + 1) * NT)
                    if b:
                        dve.wait_ge(stat_averaged, 2 * b)
                    for g in range(GROUPS):
                        last = nc.vector.bn_aggr(stat_mv[:, :, g], stat_bn[:, g, :, :])
                    last.then_inc(stat_step, 1)
                    dve.wait_ge(stat_averaged, 2 * b + 1)
                    nc.vector.tensor_copy(stat_mean[:], stat_psum[:, 0, 0:GROUPS]).then_inc(stat_step, 1)
                    dve.wait_ge(stat_step, done + 2)
                    nc.vector.tensor_tensor(stat_diff[:], stat_mv[:, 0, :], stat_mean[:], ALU.subtract).then_inc(stat_step, 1)
                    dve.wait_ge(stat_step, done + 3)
                    nc.vector.tensor_tensor(stat_diff[:], stat_diff[:], stat_diff[:], ALU.mult).then_inc(stat_step, 1)
                    dve.wait_ge(stat_step, done + 4)
                    nc.vector.tensor_tensor(stat_diff[:], stat_diff[:], stat_mv[:, 1, :], ALU.add).then_inc(stat_step, 1)
                    dve.wait_ge(stat_averaged, 2 * b + 2)
                    if b:
                        dve.wait_ge(stat_pow, b)
                    nc.vector.tensor_scalar(stat_rstd[:], stat_psum[:, 1, 0:GROUPS], GN_EPS0, None, ALU.add).then_inc(stat_step, 1)
                    dve.wait_ge(stat_pow, b + 1)
                    nc.vector.tensor_copy(gn_scale[:, b, :], stat_rstd[:])
                    nc.vector.scalar_tensor_tensor(gn_shift[:, b, :], stat_mean[:], -1.0, stat_rstd[:],
                                                   ALU.mult, ALU.mult).then_inc(stat_step, 1)

            @block.tensor
            def _(pe):
                pe.wait_ge(loaded, 16 * len(loads))
                for b in range(B):
                    pe.wait_ge(stat_step, b * steps_per_batch + 1)
                    nc.tensor.matmul(stat_psum[:, 0, 0:GROUPS], avg_all[:], stat_mv[:, 0, :],
                                     start=True, stop=True).then_inc(stat_averaged, 1)
                    pe.wait_ge(stat_step, b * steps_per_batch + 5)
                    nc.tensor.matmul(stat_psum[:, 1, 0:GROUPS], avg_all[:], stat_diff[:],
                                     start=True, stop=True).then_inc(stat_averaged, 1)

            @block.gpsimd
            def _(pool):
                pool.wait_ge(const_ready, 1)
                for b in range(B):
                    pool.wait_ge(stat_step, b * steps_per_batch + 6)
                    nc.gpsimd.tensor_tensor(stat_rstd[:], stat_rstd[:], minus_half[:], ALU.pow).then_inc(stat_pow, 1)

            @block.scalar
            def _(act):
                act.wait_ge(loaded, 16 * len(loads))
                nc.scalar.activation(decay[:], a_log[:], ACT.Exp).then_inc(act_ready, 1)
                nc.scalar.activation(skip_ident[:], ident[:], ACT.Copy, scale=skip_s[:, 0:1])
                act.wait_ge(act_ready, 1)
                nc.scalar.mul(decay[:], decay[:], -1.0)

        with ExitStack() as layer0:
            mixer_layer(nc, a, layer0, locals())
        ctx.close()
        if not debug:
            with ExitStack() as layer1:
                diffusion_layer(nc, a, layer1, ident, minus_half, x1_mv, B, H, W, C)


def mixer_layer(nc, a, ctx, env):
    (B, L, NCH, Q, KC, C, DI, KD, N, R, DT0, TAPS, HALO, x_tok, x1_dram) = (
        env[k] for k in "B L NCH Q KC C DI KD N R DT0 TAPS HALO x_tok x1_dram".split())
    (ident, select, in_w, xp_w, dt_w, out_w, proj_w, conv_w, conv_b, dt_b, skip_D, decay, ln_g, ln_b,
     proj_b, skip_ident, zeros, minus_half, gn_scale, gn_shift, x1_mv) = (
        env[k] for k in ("ident select in_w xp_w dt_w out_w proj_w conv_w conv_b dt_b skip_D decay ln_g ln_b "
                         "proj_b skip_ident zeros minus_half gn_scale gn_shift x1_mv").split())

    def sb(name, shape, dt=F32):
        return ctx.enter_context(nc.sbuf_tensor(name, shape, dt))

    signals = []

    def signal(name, per):
        s = Signal(ctx.enter_context(nc.semaphore(name)), per)
        signals.append(s)
        return s

    xt = sb("xt", [P, Q, C])
    gy = sb("gy", [P, Q, C])
    gn_now = sb("gn_now", [P, 2, 32])
    eps = sb("eps", [P, Q])
    held = sb("held", [P, 2])
    bn1 = sb("bn1", [P, Q, 6])
    mv1 = sb("mv1", [P, Q, 2])
    rstd1 = sb("rstd1", [P, Q])
    xnT = sb("xnT", [P, 2, KC, T])
    xi = sb("xi", [P, KD, HALO + T])
    zs = sb("zs", [P, KD, T])
    xs = sb("xs", [P, 2, KD, T])
    ta = sb("ta", [P, KD, T])
    tb = sb("tb", [P, KD, T])
    large = sb("large", [P, KD, T], U8)
    delta = sb("delta", [P, 2, KD, T])
    du = sb("du", [P, 2, KD, T])
    dtT = sb("dtT", [P, T])
    bc_high = sb("bc_high", [DT0, T], BF16)
    bc_mid = bc_high
    bc_rest = dtT[0:DT0, :]
    bc3 = sb("bc3", [DT0, 2, T], BF16)
    dA = sb("dA", [P, 2, KD, T + 1])
    hh = sb("hh", [P, 3, KD, T + 1])
    hc = sb("hc", [P, 2, KD, T])
    carry = sb("carry", [P, N, KD])
    c_all = sb("c_all", [P, T])
    xr = sb("xr", [P, Q, C])
    z2 = sb("z2", [P, Q, C])
    bn2 = sb("bn2", [P, Q, 6])
    mv2 = sb("mv2", [P, Q, 2])
    rstd2 = sb("rstd2", [P, Q])
    z2T = sb("z2T", [P, KC, T])
    x1 = z2T

    x1_bn = sb("x1_bn", [P, 2 * NCH, 6])
    x1_batch = sb("x1_batch", [P, 2])

    y_ps = ctx.enter_context(nc.psum_tensor("y_ps", [P, KD, T], F32))
    B_ps = ctx.enter_context(nc.psum_tensor("B_ps", [P, T], F32))
    C_ps = ctx.enter_context(nc.psum_tensor("C_ps", [P, T], F32))
    G = ctx.enter_context(nc.psum_tensor("G", [P, 2, T], F32))

    x_loaded = signal("x_loaded", 16)
    gn_scaled = signal("gn_scaled", 1)
    gn_done = signal("gn_done", 1)
    ln1_stats = signal("ln1_stats", 1)
    ln1_mv = signal("ln1_mv", 1)
    ln1_eps = signal("ln1_eps", 1)
    ln1_rstd = signal("ln1_rstd", 1)
    ln1_norm = signal("ln1_norm", 1)
    xn_T = signal("xn_T", 1)
    xn_evac = signal("xn_evac", 2)
    xi_mm = signal("xi_mm", KD)
    z_mm = signal("z_mm", KD)
    halo_moved = signal("halo_moved", 1)
    xi_evac = signal("xi_evac", KD)
    z_evac = signal("z_evac", KD)
    conv_step = signal("conv_step", KD * TAPS)
    xs_done = signal("xs_done", KD)
    xdbl_mm = signal("xdbl_mm", 1)
    dt_evac = signal("dt_evac", 1)
    bc_split = signal("bc_split", 1)
    bc_step = signal("bc_step", 3)
    bc_mid_done = signal("bc_mid_done", 2)
    dtp_mm = signal("dtp_mm", KD)
    dtp_evac = signal("dtp_evac", KD)
    sp_exp = signal("sp_exp", 2)
    sp_poly = signal("sp_poly", 2)
    sp_ln = signal("sp_ln", 2)
    series = signal("series", 4)
    chosen = signal("chosen", 4)
    delta_done = signal("delta_done", 2)
    du_done = signal("du_done", 2)
    dA_ready = signal("dA_ready", N)
    carry_loaded = signal("carry_loaded", N)
    carry_saved = signal("carry_saved", N)
    carry_zeroed = signal("carry_zeroed", 1)
    B_ready = signal("B_ready", N)
    C_ready = signal("C_ready", N)
    dBu_done = signal("dBu_done", N)
    scan_done = signal("scan_done", N)
    hC_done = signal("hC_done", N - len(POOL_STEPS))
    hC_pool = signal("hC_pool", len(POOL_STEPS))
    c_copied = signal("c_copied", len(POOL_STEPS))
    y_acc = signal("y_acc", N)
    y_evac = signal("y_evac", KD)
    yg_done = signal("yg_done", KD)
    outp_mm = signal("outp_mm", Q)
    z2_copied = signal("z2_copied", 2)
    ln2_stats = signal("ln2_stats", 1)
    ln2_mv = signal("ln2_mv", 1)
    ln2_eps = signal("ln2_eps", 1)
    ln2_rstd = signal("ln2_rstd", 1)
    ln2_norm = signal("ln2_norm", 1)
    z2_T = signal("z2_T", 1)
    z2_evac = signal("z2_evac", 2)
    xr_loaded = signal("xr_loaded", 16)
    x1_mm = signal("x1_mm", 2)
    x1_evac = signal("x1_evac", 2)
    x1_stored = signal("x1_stored", 16)
    x1_stats = signal("x1_stats", 1)
    x1_total = ctx.enter_context(nc.semaphore("x1_total"))
    gn_batch = ctx.enter_context(nc.semaphore("gn_batch"))
    zeroed = ctx.enter_context(nc.semaphore("zeroed"))

    def wait_hC(eng, t, n):
        if n in POOL_STEPS:
            wait(eng, hC_pool, t, POOL_STEPS.index(n) + 1)
        else:
            wait(eng, hC_done, t, n + 1 - sum(m < n for m in POOL_STEPS))

    def wait_state_buffer(eng, t, n):
        before = [m for m in range(n) if STATE_BUFFER[m] == STATE_BUFFER[n]]
        if before:
            wait_hC(eng, t, before[-1])
            wait(eng, carry_saved, t, before[-1] + 1)
        else:
            last = max(m for m in range(N) if STATE_BUFFER[m] == STATE_BUFFER[n])
            wait_hC(eng, t - 1, last)
            wait(eng, carry_saved, t - 1, last + 1)

    halves = [slice(0, KD // 2), slice(KD // 2, KD)]
    block = ctx.enter_context(nc.Block())

    def batch(eng, front, period, back):
        with eng.Fori(0, B) as b:
            t0 = b * NCH
            front(b, 0, t0, 0, alone=True)
            period(b, 0, t0, 0, has_back=False, has_front=True)
            with eng.Fori(0, NCH // 2 - 1) as i:
                period(b, i * 2 + 1, t0 + i * 2 + 1, 1, has_back=True, has_front=True)
                period(b, i * 2 + 2, t0 + i * 2 + 2, 0, has_back=True, has_front=True)
            period(b, NCH - 1, t0 + NCH - 1, 1, has_back=True, has_front=False)
            back(b, NCH - 1, t0 + NCH - 1, 1)

    def wait(eng, sig, t, k):
        eng.wait_ge(sig.sem, sig.of(t, k))

    @block.sync
    def _(sp):
        for s in signals:
            sp.sem_inc(s.sem, LEAD * s.per)

        def front(b, j, t, par, alone=False):
            wait(sp, gn_scaled, t - 1, 1)
            sp.dma_start(xt[:], x_tok[b, bass.ds(j * T, T), :].rearrange("(q p) c -> p q c", p=P)
                         ).then_inc(x_loaded.sem, 16)

        def load_residual(b, j, t):
            wait(sp, x1_mm, t - 1, 2)
            sp.dma_start(xr[:], x_tok[b, bass.ds(j * T, T), :].rearrange("(q p) c -> p q c", p=P)
                         ).then_inc(xr_loaded.sem, 16)

        def store(b, j, t):
            wait(sp, x1_evac, t, 2)
            sp.dma_start(x1_dram[b, :, :, bass.ds(j * T, T)].rearrange("k p t -> p k t"), x1[:]
                         ).then_inc(x1_stored.sem, 16)

        def period(b, j, t, par, has_back, has_front):
            if has_back:
                load_residual(b, j - 1, t - 1)
            if has_front:
                front(b, j + 1, t + 1, 1 - par)
            if has_back:
                store(b, j - 1, t - 1)

        def back(b, j, t, par):
            load_residual(b, j, t)
            store(b, j, t)

        batch(sp, front, period, back)
        wait(sp, x1_stored, B * NCH - 1, 16)

    @block.gpsimd
    def _(pool):
        nc.gpsimd.memset(eps[:], LN_EPS)
        nc.gpsimd.memset(dA[:, :, :, 0:1], 0.0).then_inc(zeroed, 1)
        pool.wait_ge(zeroed, 1)

        def rstd(t, mv, out, got_mv, eps_added, done):
            wait(pool, got_mv, t, 1)
            nc.gpsimd.tensor_tensor(out[:], mv[:, :, 1], eps[:], ALU.add).then_inc(eps_added.sem, 1)
            wait(pool, eps_added, t, 1)
            nc.gpsimd.tensor_tensor(out[:], out[:], minus_half[:, 0:Q], ALU.pow).then_inc(done.sem, 1)

        def groups(tile):
            return tile[:].rearrange("p q (g c) -> p q g c", g=GROUPS)

        def per_group(tile):
            return tile.unsqueeze(3).broadcast_to([P, Q, GROUPS, C // GROUPS])

        def front_norm(b, t):
            wait(pool, x_loaded, t, 16)
            wait(pool, xn_T, t - 1, 1)
            nc.gpsimd.tensor_tensor(groups(gy), groups(xt), per_group(gn_now[:, 0:1]),
                                    ALU.mult).then_inc(gn_scaled.sem, 1)
            wait(pool, gn_scaled, t, 1)
            nc.gpsimd.tensor_tensor(groups(gy), groups(gy), per_group(gn_now[:, 1:2]),
                                    ALU.add).then_inc(gn_done.sem, 1)

        def front_series(t, par, i):
            half = halves[i]
            wait(pool, sp_poly, t, i + 1)
            nc.gpsimd.tensor_tensor(ta[:, half], ta[:, half], tb[:, half], ALU.mult).then_inc(series.sem, 1)
            wait(pool, series, t, 2 * i + 1)
            nc.gpsimd.tensor_tensor(ta[:, half], ta[:, half], du[:, par, half], ALU.add).then_inc(series.sem, 1)

        def front_delta(t, par):
            for i, half in enumerate(halves):
                wait(pool, chosen, t, 2 * i + 2)
                nc.gpsimd.tensor_tensor(delta[:, par, half], delta[:, par, half], ta[:, half],
                                        ALU.add).then_inc(delta_done.sem, 1)
            for i, half in enumerate(halves):
                wait(pool, delta_done, t, i + 1)
                nc.gpsimd.tensor_tensor(du[:, par, half], delta[:, par, half], xs[:, par, half],
                                        ALU.mult).then_inc(du_done.sem, 1)

        def front_rstd(t):
            rstd(t, mv1, rstd1, ln1_mv, ln1_eps, ln1_rstd)

        def front(b, j, t, par, alone=False):
            nc.gpsimd.tensor_copy(gn_now[:, 0:1, :], gn_scale[:, bass.ds(b, 1), :])
            nc.gpsimd.tensor_copy(gn_now[:, 1:2, :], gn_shift[:, bass.ds(b, 1), :]).then_inc(gn_batch, 1)
            pool.wait_ge(gn_batch, b + 1)
            front_norm(b, t)
            front_rstd(t)
            front_series(t, par, 0)
            front_series(t, par, 1)
            front_delta(t, par)

        def gate(t, par):
            wait(pool, z_evac, t, KD)
            for m in range(KD):
                wait(pool, y_evac, t, m + 1)
                nc.gpsimd.tensor_tensor(xs[:, par, m], xs[:, par, m], zs[:, m], ALU.mult).then_inc(yg_done.sem, 1)

        def back_rstd(t):
            rstd(t, mv2, rstd2, ln2_mv, ln2_eps, ln2_rstd)

        def make_hC(t, n):
            wait(pool, scan_done, t, n + 1)
            wait(pool, c_copied, t, POOL_STEPS.index(n) + 1)
            if n >= 2:
                wait(pool, y_acc, t, n - 1)
            else:
                wait(pool, y_acc, t - 1, N - 1 + n)
            nc.gpsimd.tensor_tensor(hc[:, n % 2], hh[:, STATE_BUFFER[n], :, 1:T + 1],
                                    c_all[:].unsqueeze(1).broadcast_to([P, KD, T]), ALU.mult).then_inc(hC_pool.sem, 1)

        def period(b, j, t, par, has_back, has_front):
            for n in range(N):
                if has_front and n == 1:
                    front_rstd(t + 1)
                if n in POOL_STEPS:
                    make_hC(t, n)
                if has_front and n == 0:
                    front_norm(b, t + 1)
                if has_back and n == 0:
                    gate(t - 1, 1 - par)
                if has_back and n == 4:
                    back_rstd(t - 1)
                if has_front and n == 10:
                    front_series(t + 1, 1 - par, 0)
                if has_front and n == 12:
                    front_series(t + 1, 1 - par, 1)
                if has_front and n == 14:
                    front_delta(t + 1, 1 - par)

        def back(b, j, t, par):
            gate(t, par)
            back_rstd(t)

        batch(pool, front, period, back)

    @block.scalar
    def _(act):
        act.wait_ge(zeroed, 1)

        def scan_step(t, par, n):
            buf = n % 2
            if n == 0:
                wait(act, delta_done, t, 2)
            if n >= 2:
                wait(act, scan_done, t, n - 1)
            else:
                wait(act, scan_done, t - 1, N - 1 + n)
            for m in range(KD):
                last = nc.scalar.activation(dA[:, buf, m, 1:T + 1], delta[:, par, m], ACT.Exp,
                                            scale=decay[:, m, n:n + 1])
            last.then_inc(dA_ready.sem, 1)
            if n - 1 in POOL_STEPS:
                copy_C(t, n - 1)
            wait_state_buffer(act, t, n)
            nc.scalar.copy(hh[:, STATE_BUFFER[n], :, 0], carry[:, n, :]).then_inc(carry_loaded.sem, 1)
            if n:
                save_carry(t, n - 1)

        def copy_C(t, n):
            i = POOL_STEPS.index(n)
            wait(act, C_ready, t, n + 1)
            if i:
                wait(act, hC_pool, t, i)
            else:
                wait(act, hC_pool, t - 1, len(POOL_STEPS))
            nc.scalar.copy(c_all[:], C_ps[:]).then_inc(c_copied.sem, 1)

        def save_carry(t, n):
            wait(act, scan_done, t, n + 1)
            wait(act, carry_loaded, t, n + 1)
            nc.scalar.copy(carry[:, n, :], hh[:, STATE_BUFFER[n], :, T]).then_inc(carry_saved.sem, 1)

        def front_xn(t, par):
            wait(act, xn_T, t, 1)
            for k in range(KC):
                nc.scalar.activation(xnT[:, par, k], G[:, k], ACT.Identity, bias=ln_b[:, k:k + 1],
                                     scale=ln_g[:, k:k + 1]).then_inc(xn_evac.sem, 1)

        def front_halo(t, first):
            wait(act, conv_step, t - 1, KD * TAPS)
            wait(act, xi_evac, t - 1, KD)
            if first:
                nc.scalar.copy(xi[:, :, 0:HALO], zeros[:, 0:KD * HALO].rearrange("p (k h) -> p k h", h=HALO)
                               ).then_inc(halo_moved.sem, 1)
            else:
                nc.scalar.copy(xi[:, :, 0:HALO], xi[:, :, T:T + HALO]).then_inc(halo_moved.sem, 1)

        def front_xi(t, m0, m1):
            if m0 == 0:
                wait(act, halo_moved, t, 1)
            for m in range(m0, m1):
                wait(act, xi_mm, t, m + 1)
                nc.scalar.copy(xi[:, m, HALO:], G[:, m % 2]).then_inc(xi_evac.sem, 1)

        def gate_silu(t, m0, m1):
            if m0 == 0:
                wait(act, yg_done, t - 1, KD)
            for m in range(m0, m1):
                wait(act, z_mm, t, m + 1)
                nc.scalar.activation(zs[:, m], G[:, m % 2], ACT.Silu).then_inc(z_evac.sem, 1)

        def front_silu(t, par):
            wait(act, outp_mm, t - 2, Q)
            for m in range(KD):
                wait(act, conv_step, t, 2 * TAPS * (m // 2) + 2 * (TAPS - 1) + m % 2 + 1)
                nc.scalar.activation(xs[:, par, m], ta[:, m], ACT.Silu).then_inc(xs_done.sem, 1)

        def front_bc(t, par):
            wait(act, xdbl_mm, t, 1)
            nc.scalar.copy(dtT[DT0:DT0 + R, :], G[DT0:DT0 + R, 0]).then_inc(dt_evac.sem, 1)
            nc.scalar.copy(bc3[0:2 * N, par], G[0:2 * N, 0])
            nc.scalar.copy(bc_high[:], G[0:DT0, 0]).then_inc(bc_split.sem, 1)

        def front_dt(t, par, m0, m1):
            for m in range(m0, m1):
                wait(act, dtp_mm, t, m + 1)
                v = G[:, (m + 1) % 2]
                nc.scalar.activation(du[:, par, m], v, ACT.Abs, bias=dt_b[:, m:m + 1])
                nc.scalar.activation(delta[:, par, m], v, ACT.Relu, bias=dt_b[:, m:m + 1]).then_inc(dtp_evac.sem, 1)

        def front_softplus(t, par, i):
            half = halves[i]
            wait(act, dtp_evac, t, KD // 2 * (i + 1))
            nc.scalar.activation(du[:, par, half], du[:, par, half], ACT.Exp, scale=-1.0).then_inc(sp_exp.sem, 1)
            wait(act, sp_exp, t, i + 1)
            if i == 0:
                wait(act, delta_done, t - 1, 2)
                wait(act, xs_done, t, KD)
            nc.scalar.activation(ta[:, half], du[:, par, half], ACT.Copy, bias=-0.5, scale=1.0 / 3)
            nc.scalar.activation(tb[:, half], du[:, par, half], ACT.Square).then_inc(sp_poly.sem, 1)

        def front_ln(t, par, i):
            wait(act, series, t, 2 * i + 1)
            nc.scalar.activation(tb[:, halves[i]], du[:, par, halves[i]], ACT.Ln, bias=1.0).then_inc(sp_ln.sem, 1)

        def back_copy(t, q0, q1):
            if q0 == 0:
                wait(act, z2_T, t - 1, 1)
            for i in range(q0 // 2, q1 // 2):
                wait(act, outp_mm, t, 2 * i + 2)
                nc.scalar.copy(z2[:, 2 * i:2 * i + 2, :].rearrange("p q c -> p (q c)"), G[:, i]
                               ).then_inc(z2_copied.sem, 1)

        def back_z2(t):
            wait(act, z2_T, t, 1)
            wait(act, x1_stored, t - 1, 16)
            wait(act, x1_stats, t - 1, 1)
            for k in range(KC):
                nc.scalar.activation(z2T[:, k], G[:, k], ACT.Identity, bias=ln_b[:, k:k + 1],
                                     scale=ln_g[:, k:k + 1]).then_inc(z2_evac.sem, 1)

        def back_x1(t):
            wait(act, x1_mm, t, KC)
            for k in range(KC):
                nc.scalar.activation(x1[:, k], G[:, k], ACT.Identity, bias=proj_b[:, k:k + 1]
                                     ).then_inc(x1_evac.sem, 1)

        def front(b, j, t, par, alone=False):
            wait(act, carry_saved, t - 1, N)
            nc.scalar.copy(carry[:].rearrange("p n k -> p (n k)"), zeros[:]).then_inc(carry_zeroed.sem, 1)
            act.wait_ge(carry_zeroed.sem, b + (LEAD + 1))
            front_xn(t, par)
            front_halo(t, True)
            front_xi(t, 0, KD)
            front_silu(t, par)
            front_bc(t, par)
            for i in range(2):
                front_dt(t, par, 2 * i, 2 * i + 2)
                front_softplus(t, par, i)
            for i in range(2):
                front_ln(t, par, i)

        def period(b, j, t, par, has_back, has_front):
            for n in range(N):
                scan_step(t, par, n)
                f, fp, u = t + 1, 1 - par, t - 1
                if has_back:
                    if n == 2:
                        back_copy(u, 0, 2)
                    if n == 3:
                        back_copy(u, 2, 4)
                if has_front:
                    if n == 4:
                        front_xn(f, fp)
                        front_halo(f, False)
                    if n == 5:
                        front_xi(f, 0, 2)
                    if n == 6:
                        front_xi(f, 2, 4)
                    if n == 7:
                        front_silu(f, fp)
                    if n == 8:
                        front_bc(f, fp)
                    if n == 10:
                        front_dt(f, fp, 0, 2)
                        front_softplus(f, fp, 0)
                    if n == 11:
                        front_dt(f, fp, 2, 4)
                        front_softplus(f, fp, 1)
                    if n == 13:
                        front_ln(f, fp, 0)
                        front_ln(f, fp, 1)
                if n == 12:
                    gate_silu(t, 0, 2)
                if n == 13:
                    gate_silu(t, 2, 4)
                if has_back:
                    if n == 14:
                        back_z2(u)
                    if n == 15:
                        back_x1(u)
            save_carry(t, N - 1)

        def back(b, j, t, par):
            back_copy(t, 0, Q)
            back_z2(t)
            back_x1(t)

        batch(act, front, period, back)

    @block.vector
    def _(dve):
        def make_dBu(t, par, n):
            buf = STATE_BUFFER[n]
            if n == 0:
                wait(dve, du_done, t, 2)
            wait(dve, B_ready, t, n + 1)
            wait_state_buffer(dve, t, n)
            nc.vector.tensor_tensor(hh[:, buf, :, 1:T + 1], du[:, par],
                                    B_ps[:].unsqueeze(1).broadcast_to([P, KD, T]), ALU.mult).then_inc(dBu_done.sem, 1)

        def scan(t, n):
            buf = STATE_BUFFER[n]
            wait(dve, dA_ready, t, n + 1)
            wait(dve, carry_loaded, t, n + 1)
            wait(dve, dBu_done, t, n + 1)
            states = hh[:, buf].rearrange("p k t -> p (k t)")
            nc.vector.tensor_tensor_scan(states, dA[:, n % 2].rearrange("p k t -> p (k t)"), states, 0.0,
                                         ALU.mult, ALU.add).then_inc(scan_done.sem, 1)

        def make_hC(t, n):
            wait(dve, C_ready, t, n + 1)
            wait(dve, scan_done, t, n + 1)
            if n >= 2:
                wait(dve, y_acc, t, n - 1)
            else:
                wait(dve, y_acc, t - 1, N - 1 + n)
            nc.vector.tensor_tensor(hc[:, n % 2], hh[:, STATE_BUFFER[n], :, 1:T + 1],
                                    C_ps[:].unsqueeze(1).broadcast_to([P, KD, T]), ALU.mult).then_inc(hC_done.sem, 1)

        def hold():
            nc.vector.memset(held[:, 0:1], 0.0)

        def moments(t, src, bn, mv, stats, got_mv):
            for q in range(Q):
                last = nc.vector.bn_stats(bn[:, q, :], src(q))
            last.then_inc(stats.sem, 1)
            wait(dve, stats, t, 1)
            hold()
            for q in range(Q):
                last = nc.vector.bn_aggr(mv[:, q, :], bn[:, q, :])
            last.then_inc(got_mv.sem, 1)

        def front_moments(t):
            wait(dve, gn_done, t, 1)
            moments(t, lambda q: gy[:, q, :], bn1, mv1, ln1_stats, ln1_mv)

        def front_norm(t):
            wait(dve, ln1_rstd, t, 1)
            for q in range(Q):
                last = nc.vector.tensor_scalar(gy[:, q, :], gy[:, q, :], mv1[:, q, 0:1], rstd1[:, q:q + 1],
                                               ALU.subtract, ALU.mult)
            last.then_inc(ln1_norm.sem, 1)

        def front_conv(t, m0, m1):
            if m0 == 0:
                wait(dve, delta_done, t - 1, 2)
            for m in range(m0, m1):
                wait(dve, xi_evac, t, m + 1)
                nc.vector.tensor_scalar(ta[:, m], xi[:, m, 0:T], conv_w[:, m, 0:1], conv_b[:, m:m + 1],
                                        ALU.mult, ALU.add).then_inc(conv_step.sem, 1)
            first = m0 * TAPS
            for tap in range(1, TAPS):
                for m in range(m0, m1):
                    wait(dve, conv_step, t, first + (m1 - m0) * (tap - 1) + m - m0 + 1)
                    nc.vector.scalar_tensor_tensor(ta[:, m], xi[:, m, tap:tap + T], conv_w[:, m, tap:tap + 1],
                                                   ta[:, m], ALU.mult, ALU.add).then_inc(conv_step.sem, 1)

        def front_bc(t, par):
            wait(dve, bc_split, t, 1)
            nc.vector.tensor_tensor(bc_rest, G[0:DT0, 0], bc_high[:], ALU.subtract).then_inc(bc_step.sem, 1)
            wait(dve, bc_step, t, 1)
            nc.vector.tensor_copy(bc_mid[:], bc_rest).then_inc(bc_step.sem, 1)
            nc.vector.tensor_copy(bc3[2 * N:4 * N, par], dtT[2 * N:4 * N, :])
            wait(dve, bc_step, t, 2)
            nc.vector.tensor_tensor(bc3[4 * N:6 * N, par], dtT[4 * N:6 * N, :], bc_mid[4 * N:6 * N, :],
                                    ALU.subtract).then_inc(bc_step.sem, 1)

        def front_choose(t, par, i):
            half = halves[i]
            wait(dve, sp_exp, t, i + 1)
            nc.vector.tensor_scalar(large[:, half], du[:, par, half], SERIES_BELOW, None, ALU.is_ge).then_inc(chosen.sem, 1)
            wait(dve, chosen, t, 2 * i + 1)
            wait(dve, sp_ln, t, i + 1)
            wait(dve, series, t, 2 * i + 2)
            hold()
            nc.vector.copy_predicated(ta[:, half], large[:, half], tb[:, half]).then_inc(chosen.sem, 1)

        def y_out(t, par):
            wait(dve, y_acc, t, N)
            for m in range(KD):
                nc.vector.scalar_tensor_tensor(xs[:, par, m], xs[:, par, m], skip_D[:, m:m + 1], y_ps[:, m],
                                               ALU.mult, ALU.add).then_inc(y_evac.sem, 1)

        def back_moments(t):
            wait(dve, z2_copied, t, 2)
            moments(t, lambda q: z2[:, q, :], bn2, mv2, ln2_stats, ln2_mv)

        def back_norm(t):
            wait(dve, ln2_rstd, t, 1)
            for q in range(Q):
                last = nc.vector.tensor_scalar(z2[:, q, :], z2[:, q, :], mv2[:, q, 0:1], rstd2[:, q:q + 1],
                                               ALU.subtract, ALU.mult)
            last.then_inc(ln2_norm.sem, 1)

        def back_stats(j, t):
            wait(dve, x1_evac, t, 2)
            for k in range(KC):
                last = nc.vector.bn_stats(x1_bn[:, bass.ds(j * 2 + k, 1), :], x1[:, k])
            last.then_inc(x1_stats.sem, 1)

        def front(b, j, t, par, alone=False):
            front_moments(t)
            front_norm(t)
            front_conv(t, 0, 2)
            front_conv(t, 2, 4)
            front_bc(t, par)
            front_choose(t, par, 0)
            front_choose(t, par, 1)

        def period(b, j, t, par, has_back, has_front):
            f, fp, u = t + 1, 1 - par, t - 1
            make_dBu(t, par, 0)
            for n in range(N):
                scan(t, n)
                if has_back and n == 0:
                    y_out(u, fp)
                if n < N - 1:
                    make_dBu(t, par, n + 1)
                if n not in POOL_STEPS:
                    make_hC(t, n)
                if has_front:
                    if n == 0:
                        front_moments(f)
                    if n == 1:
                        front_norm(f)
                    if n == 5:
                        front_conv(f, 0, 2)
                    if n == 6:
                        front_conv(f, 2, 4)
                    if n == 8:
                        front_bc(f, fp)
                    if n == 12:
                        front_choose(f, fp, 0)
                    if n == 13:
                        front_choose(f, fp, 1)
                if has_back:
                    if n == 3:
                        back_moments(u)
                    if n == 4:
                        back_norm(u)
                    if n == 15:
                        back_stats(j - 1, u)

        def back(b, j, t, par):
            y_out(t, par)
            back_moments(t)
            back_norm(t)
            back_stats(j, t)
            wait(dve, x1_stats, t, 1)
            hold()
            nc.vector.bn_aggr(x1_batch[:], x1_bn[:].rearrange("p n s -> p (n s)")).then_inc(x1_total, 1)
            dve.wait_ge(x1_total, b * 2 + 1)
            nc.vector.tensor_copy(x1_mv[:, :, bass.ds(b, 1)], x1_batch[:].unsqueeze(2)).then_inc(x1_total, 1)
            dve.wait_ge(x1_total, b * 2 + 2)

        batch(dve, front, period, back)

    @block.tensor
    def _(pe):
        def spread_B(t, par, n):
            if n == 0:
                wait(pe, bc_step, t, 3)
            wait(pe, dBu_done, t, n)
            nc.tensor.matmul(B_ps[:], select[:, n, :], bc3[:, par], start=True, stop=True).then_inc(B_ready.sem, 1)

        def spread_C(t, par, n):
            if n == 0:
                wait_hC(pe, t - 1, N - 1)
            elif n - 1 in POOL_STEPS:
                wait(pe, c_copied, t, POOL_STEPS.index(n - 1) + 1)
            else:
                wait_hC(pe, t, n - 1)
            nc.tensor.matmul(C_ps[:], select[:, N + n, :], bc3[:, par], start=True, stop=True).then_inc(C_ready.sem, 1)

        def add_y(t, n):
            if n == 0:
                wait(pe, y_evac, t - 1, KD)
            wait_hC(pe, t, n)
            for m in range(KD):
                last = nc.tensor.matmul(y_ps[:, m], ident[:], hc[:, n % 2, m], start=(n == 0), stop=(n == N - 1))
            last.then_inc(y_acc.sem, 1)

        def front_T(t, alone, after_back):
            wait(pe, ln1_norm, t, 1)
            if alone:
                wait(pe, x1_evac, t - 1, 2)
            elif after_back:
                wait(pe, z2_copied, t - 2, 2)
            else:
                wait(pe, dtp_evac, t - 1, KD)
            for k in range(KC):
                for q in range(Q):
                    last = nc.tensor.transpose(G[:, k, q * P:(q + 1) * P], gy[:, q, k * P:(k + 1) * P], ident[:])
            last.then_inc(xn_T.sem, 1)

        def front_xi(t, par, m0, m1):
            for m in range(m0, m1):
                if m < 2:
                    wait(pe, xn_evac, t, 2)
                else:
                    wait(pe, xi_evac, t, m - 1)
                for k in range(KC):
                    last = nc.tensor.matmul(G[:, m % 2], in_w[:, k, m * P:(m + 1) * P], xnT[:, par, k],
                                            start=(k == 0), stop=(k == KC - 1))
                last.then_inc(xi_mm.sem, 1)

        def gate_z(t, par, m0, m1, has_front):
            for m in range(m0, m1):
                if m >= 2:
                    wait(pe, z_evac, t, m - 1)
                elif has_front:
                    wait(pe, dtp_evac, t + 1, KD)
                else:
                    wait(pe, z2_copied, t - 1, 2)
                for k in range(KC):
                    last = nc.tensor.matmul(G[:, m % 2], in_w[:, k, (KD + m) * P:(KD + m + 1) * P], xnT[:, par, k],
                                            start=(k == 0), stop=(k == KC - 1))
                last.then_inc(z_mm.sem, 1)

        def front_xdbl(t, par):
            wait(pe, xi_evac, t, KD)
            for m in range(KD):
                wait(pe, xs_done, t, m + 1)
                last = nc.tensor.matmul(G[0:DT0 + R, 0], xp_w[:, m, :], xs[:, par, m], start=(m == 0), stop=(m == KD - 1))
            last.then_inc(xdbl_mm.sem, 1)

        def front_dt(t, m0, m1):
            wait(pe, dt_evac, t, 1)
            for m in range(m0, m1):
                if m == 1:
                    wait(pe, bc_split, t, 1)
                    wait(pe, bc_step, t, 1)
                if m >= 2:
                    wait(pe, dtp_evac, t, m - 1)
                nc.tensor.matmul(G[:, (m + 1) % 2], dt_w[DT0:DT0 + R, m * P:(m + 1) * P], dtT[DT0:DT0 + R, :],
                                 start=True, stop=True).then_inc(dtp_mm.sem, 1)

        def back_out(t, par, q0, q1):
            if q0 == 0:
                wait(pe, yg_done, t, KD)
                wait(pe, x1_evac, t - 1, 2)
                wait(pe, z_evac, t, KD)
            for q in range(q0, q1):
                o = G[:, q // 2, (q % 2) * C:(q % 2 + 1) * C]
                for m in range(KD):
                    last = nc.tensor.matmul(o, xs[:, par, m, q * P:(q + 1) * P], out_w[:, m, :],
                                            start=(m == 0), stop=(m == KD - 1))
                    for k in range(KC if m == 0 else 0):
                        nc.tensor.matmul(G[:, q // 2, (q % 2) * C + k * P:(q % 2) * C + (k + 1) * P],
                                         xnT[:, par, k, q * P:(q + 1) * P], skip_ident[:],
                                         start=False, stop=False, skip_group_check=True)
                last.then_inc(outp_mm.sem, 1)

        def back_T(t, after_z):
            wait(pe, ln2_norm, t, 1)
            if after_z:
                wait(pe, z_evac, t + 1, KD)
            for k in range(KC):
                for q in range(Q):
                    last = nc.tensor.transpose(G[:, k, q * P:(q + 1) * P], z2[:, q, k * P:(k + 1) * P], ident[:])
            last.then_inc(z2_T.sem, 1)

        def back_proj(t, k0, k1):
            if k0 == 0:
                wait(pe, z2_evac, t, 2)
                wait(pe, xr_loaded, t, 16)
            for k in range(k0, k1):
                for c in range(KC):
                    last = nc.tensor.matmul(G[:, k], proj_w[:, c, bass.ds(k, P, KC)], z2T[:, c],
                                            start=(c == 0), stop=(c == KC - 1))
                    for q in range(Q if c == 0 else 0):
                        nc.tensor.matmul(G[:, k, q * P:(q + 1) * P], xr[:, q, bass.ds(k, P, KC)], ident[:],
                                         start=False, stop=False, skip_group_check=True)
                last.then_inc(x1_mm.sem, 1)

        def front(b, j, t, par, alone=False):
            front_T(t, True, False)
            front_xi(t, par, 0, KD)
            front_xdbl(t, par)
            front_dt(t, 0, KD)
            spread_B(t, par, 0)

        def period(b, j, t, par, has_back, has_front):
            f, fp, u = t + 1, 1 - par, t - 1
            for n in range(N):
                if n < N - 1:
                    spread_B(t, par, n + 1)
                spread_C(t, par, n)
                if n and n - 1 not in POOL_STEPS:
                    add_y(t, n - 1)
                if has_back:
                    if n == 1:
                        back_out(u, fp, 0, 2)
                    if n == 2:
                        back_out(u, fp, 2, 4)
                if has_front:
                    if n == 3:
                        front_T(f, False, has_back)
                    if n == 4:
                        front_xi(f, fp, 0, 2)
                    if n == 5:
                        front_xi(f, fp, 2, 4)
                    if n == 7:
                        front_xdbl(f, fp)
                    if n == 9:
                        front_dt(f, 0, 2)
                    if n == 10:
                        front_dt(f, 2, 4)
                if n == 11:
                    gate_z(t, par, 0, 2, has_front)
                if n == 12:
                    gate_z(t, par, 2, 4, has_front)
                if has_back:
                    if n == 13:
                        back_T(u, True)
                    if n == 14:
                        back_proj(u, 0, KC)
                if n - 1 in POOL_STEPS:
                    add_y(t, n - 1)
            add_y(t, N - 1)
            if has_front:
                spread_B(f, fp, 0)

        def back(b, j, t, par):
            back_out(t, par, 0, Q)
            back_T(t, False)
            back_proj(t, 0, KC)

        batch(pe, front, period, back)


K_STEPS, DT, BN_EPS, GN_EPS1 = 5, 0.2, 1e-3, 1e-5
ROWS = 4


def diffusion_layer(nc, a, ctx, ident, minus_half, x1_mv, B, H, W, C):
    KC = C // P
    NR = H // ROWS
    M = ROWS * W
    assert W == P and M == T and KC == 2 and NR % 2 == 0 and NR >= 6
    x1_dram = a["x1_dram"]
    x1_rows = x1_dram.rearrange("b k p (h w) -> b p k h w", w=W)
    out_tok = a["out"].rearrange("b h w c -> b (h w) c")

    def sb(name, shape, dt=F32):
        return ctx.enter_context(nc.sbuf_tensor(name, shape, dt))

    signals = []

    def signal(name, per):
        s = Signal(ctx.enter_context(nc.semaphore(name)), per)
        signals.append(s)
        return s

    def wait(eng, sig, t, k):
        eng.wait_ge(sig.sem, sig.of(t, k))

    avg4 = sb("avg4", [P, P])
    up_one = sb("up_one", [P, P])
    down_one = sb("down_one", [P, P])
    taps_w = sb("taps_w", [P, 2, 9, KC])
    taps = sb("taps", [P, 2, KC, 9, P])
    bn_in = sb("bn_in", [P, 3, 4, KC])
    bn_s = sb("bn_s", [P, 3, KC])
    bn_b = sb("bn_b", [P, 3, KC])
    g2_mean = sb("g2_mean", [P, B])
    g2_var = sb("g2_var", [P, B])
    g2_scale = sb("g2_scale", [P, B])
    g2_shift = sb("g2_shift", [P, B])
    one = sb("one", [P, 1])
    g2_now = sb("g2_now", [P, 2])

    with (
        nc.psum_tensor("g2_psum", [P, 2, 512], F32) as g2_psum,
        nc.semaphore("c_loaded") as c_loaded,
        nc.semaphore("c_step") as c_step,
        nc.semaphore("c_mean") as c_mean,
        nc.semaphore("c_pow") as c_pow,
        nc.Block() as block,
    ):
        @block.sync
        def _(sp):
            for dst, src in ((avg4, "avg4"), (up_one, "up_one"), (down_one, "down_one"), (taps_w, "taps_w"), (bn_in, "bn_in")):
                sp.dma_start(dst[:], a[src]).then_inc(c_loaded, 16)

        @block.vector
        def _(dve):
            nc.vector.memset(one[:], 1.0)
            dve.wait_ge(c_loaded, 16 * 5)
            for c in range(2):
                for k in range(KC):
                    for i in range(9):
                        nc.vector.tensor_scalar(taps[:, c, k, i, :], ident[:], taps_w[:, c, i, k:k + 1], None, ALU.mult)
            nc.vector.tensor_scalar(bn_s[:], bn_in[:, :, 3, :], BN_EPS, None, ALU.add).then_inc(c_step, 1)
            dve.wait_ge(c_pow, 1)
            nc.vector.tensor_tensor(bn_s[:], bn_s[:], bn_in[:, :, 0, :], ALU.mult).then_inc(c_step, 1)
            dve.wait_ge(c_step, 2)
            nc.vector.tensor_tensor(bn_b[:], bn_in[:, :, 2, :], bn_s[:], ALU.mult).then_inc(c_step, 1)
            dve.wait_ge(c_step, 3)
            nc.vector.tensor_tensor(bn_b[:], bn_in[:, :, 1, :], bn_b[:], ALU.subtract).then_inc(c_step, 1)
            dve.wait_ge(c_step, 4)
            nc.vector.tensor_scalar(bn_s[:, 0:2, :], bn_s[:, 0:2, :], DT, None, ALU.mult)
            nc.vector.tensor_scalar(bn_b[:, 0:2, :], bn_b[:, 0:2, :], DT, None, ALU.mult)
            dve.wait_ge(c_mean, 1)
            nc.vector.tensor_copy(g2_mean[:], g2_psum[:, 0, 0:B]).then_inc(c_step, 1)
            dve.wait_ge(c_step, 5)
            nc.vector.tensor_tensor(g2_var[:], x1_mv[:, 0, :], g2_mean[:], ALU.subtract).then_inc(c_step, 1)
            dve.wait_ge(c_step, 6)
            nc.vector.tensor_tensor(g2_var[:], g2_var[:], g2_var[:], ALU.mult).then_inc(c_step, 1)
            dve.wait_ge(c_step, 7)
            nc.vector.tensor_tensor(g2_var[:], g2_var[:], x1_mv[:, 1, :], ALU.add).then_inc(c_step, 1)
            dve.wait_ge(c_mean, 2)
            nc.vector.tensor_scalar(g2_scale[:], g2_psum[:, 1, 0:B], GN_EPS1, None, ALU.add).then_inc(c_step, 1)
            dve.wait_ge(c_pow, 2)
            nc.vector.scalar_tensor_tensor(g2_shift[:], g2_mean[:], -1.0, g2_scale[:], ALU.mult, ALU.mult)

        @block.tensor
        def _(pe):
            pe.wait_ge(c_loaded, 16 * 5)
            nc.tensor.matmul(g2_psum[:, 0, 0:B], avg4[:], x1_mv[:, 0, :], start=True, stop=True).then_inc(c_mean, 1)
            pe.wait_ge(c_step, 8)
            nc.tensor.matmul(g2_psum[:, 1, 0:B], avg4[:], g2_var[:], start=True, stop=True).then_inc(c_mean, 1)

        @block.gpsimd
        def _(pool):
            half = minus_half[:, 0:3 * KC].rearrange("p (a k) -> p a k", k=KC)
            pool.wait_ge(c_step, 1)
            nc.gpsimd.tensor_tensor(bn_s[:], bn_s[:], half, ALU.pow).then_inc(c_pow, 1)
            pool.wait_ge(c_step, 9)
            nc.gpsimd.tensor_tensor(g2_scale[:], g2_scale[:], minus_half[:, 0:B], ALU.pow).then_inc(c_pow, 1)

    xh = sb("xh", [P, KC, ROWS + 2, W])
    sn = sb("sn", [P, KC, ROWS + 2, W + 2])
    hs = sb("hs", [P, 2, KC, ROWS, W + 2])
    ax = sb("ax", [P, KC, ROWS, W + 2])
    ay = sb("ay", [P, KC, ROWS, W])
    sum_w = sb("sum_w", [P, KC, ROWS + 2, W])
    dif_w = sb("dif_w", [P, KC, ROWS + 2, W])
    gy = sb("gy2", [P, KC, ROWS, W])
    gx = sb("gx2", [P, KC, ROWS, W])
    pq = sb("pq", [P, KC, ROWS, W])
    den = sb("den", [P, KC, ROWS, W])
    rec = sb("rec", [P, KC, ROWS, W])
    dd = sb("dd", [P, KC, ROWS, W])
    dbx = sb("dbx", [P, KC, ROWS, W])
    dby = sb("dby", [P, KC, ROWS, W])
    c_old = sb("c_old", [P, 2, KC, ROWS, W])
    c_own = sb("c_own", [P, 2, KC, ROWS, W])
    c_left = sb("c_left", [P, 2, KC, ROWS, W])
    c_right = sb("c_right", [P, 2, KC, ROWS, W])
    c_moved = sb("c_moved", [P, 2, KC, ROWS, W])
    c_same = sb("c_same", [P, 2, KC, ROWS, W])
    src = sb("src", [P, 2, KC, ROWS, W])
    src1 = sb("src1", [P, KC, ROWS, W])
    src2 = sb("src2", [P, KC, ROWS, W])
    hb = sb("hb", [P, 3, KC, ROWS, W + 2])
    q_old = sb("q_old", [P, KC, ROWS, W])
    q_own = sb("q_own", [P, KC, ROWS, W])
    q_left = sb("q_left", [P, KC, ROWS, W])
    q_right = sb("q_right", [P, KC, ROWS, W])
    q_moved = sb("q_moved", [P, KC, ROWS, W])
    q_same = sb("q_same", [P, KC, ROWS, W])
    xres = sb("xres", [P, KC, ROWS, W])
    fo = sb("fo", [P, KC, ROWS, W])
    ot = sb("ot", [P, ROWS, C])

    acc_ps = ctx.enter_context(nc.psum_tensor("acc_ps", [P, KC, ROWS, W], F32))
    moved_ps = ctx.enter_context(nc.psum_tensor("moved_ps", [P, KC, ROWS, W], F32))
    conv_ps = ctx.enter_context(nc.psum_tensor("conv_ps", [P, 2 * KC, ROWS, W], F32))

    xh_loaded = signal("xh_loaded", 32)
    sn_done = signal("sn_done", 1)
    hs_done = signal("hs_done", 1)
    conv_mm = signal("conv_mm", 2 * KC)
    ax_done = signal("ax_done", 1)
    ay_done = signal("ay_done", 1)
    ay_moved = signal("ay_moved", 1)
    ay_used = signal("ay_used", 1)
    sums_done = signal("sums_done", 2)
    sob = signal("sob", 4)
    squared = signal("squared", 2)
    den_log = signal("den_log", 1)
    rec_done = signal("rec_done", 1)
    coef = signal("coef", 8)
    da_done = signal("da_done", 3)
    e2_done = signal("e2_done", 4)
    src_done = signal("src_done", 1)
    dv_done = signal("dv_done", 2)
    old_done = signal("old_done", 2)
    src_steps = signal("src_steps", 4)
    q_old_done = signal("q_old_done", 2 * (K_STEPS - 2))
    q_own_done = signal("q_own_done", K_STEPS - 1)
    q_pool_done = signal("q_pool_done", len(POOL_SUMS))
    q_left_done = signal("q_left_done", K_STEPS)
    q_sides_done = signal("q_sides_done", len(SIDE_SUMS))
    q_right_done = signal("q_right_done", K_STEPS)
    q_same_done = signal("q_same_done", K_STEPS)
    q_moved_done = signal("q_moved_done", 2 * K_STEPS)
    moved = signal("moved", K_STEPS)
    acc_done = signal("acc_done", K_STEPS)
    h_done = signal("h_done", K_STEPS)
    wrapped = signal("wrapped", K_STEPS)
    xres_loaded = signal("xres_loaded", 16)
    fo_done = signal("fo_done", 1)
    added = signal("added", 1)
    fo_T = signal("fo_T", 1)
    ot_done = signal("ot_done", 1)
    out_stored = signal("out_stored", 16)

    def state(par, it):
        return hs[:, par] if it == 0 else hb[:, (it - 1) % 3]

    batch_norm = ctx.enter_context(nc.semaphore("batch_norm"))

    def flat(t):
        return t.rearrange("p k r w -> p k (r w)")

    block = ctx.enter_context(nc.Block())

    def batch(eng, prep, period, finish):
        with eng.Fori(0, B) as b:
            u0 = b * NR
            prep(b, 0, u0, 0, top=True)
            period(b, 0, u0, 0, finishes=False, prepares=True)
            with eng.Fori(0, NR // 2 - 2) as i:
                period(b, i * 2 + 1, u0 + i * 2 + 1, 1, finishes=True, prepares=True)
                period(b, i * 2 + 2, u0 + i * 2 + 2, 0, finishes=True, prepares=True)
            period(b, NR - 3, u0 + NR - 3, 1, finishes=True, prepares=True)
            period(b, NR - 2, u0 + NR - 2, 0, finishes=True, prepares=True, bottom=True)
            period(b, NR - 1, u0 + NR - 1, 1, finishes=True, prepares=False)
            finish(b, NR - 1, u0 + NR - 1)

    @block.sync
    def _(sp):
        for s in signals:
            sp.sem_inc(s.sem, LEAD * s.per)

        def prep(b, r, u, par, top=False, bottom=False):
            wait(sp, hs_done, u - 1, 1)
            if top:
                sp.dma_start(xh[:, :, 1:], x1_rows[b, :, :, 0:ROWS + 1, :]).then_inc(xh_loaded.sem, 16)
                sp.dma_start(xh[:, :, 0:1], x1_rows[b, :, :, 1:2, :]).then_inc(xh_loaded.sem, 16)
            elif bottom:
                sp.dma_start(xh[:, :, 0:ROWS + 1], x1_rows[b, :, :, H - ROWS - 1:H, :]).then_inc(xh_loaded.sem, 16)
                sp.dma_start(xh[:, :, ROWS + 1:], x1_rows[b, :, :, H - 2:H - 1, :]).then_inc(xh_loaded.sem, 16)
            else:
                for k in range(KC):
                    sp.dma_start(xh[:, k], x1_rows[b, :, k, bass.ds(r * ROWS - 1, ROWS + 2), :]
                                 ).then_inc(xh_loaded.sem, 16)

        def load_residual(b, r, u):
            wait(sp, added, u - 1, 1)
            sp.dma_start(xres[:], x1_rows[b, :, :, bass.ds(r * ROWS, ROWS), :]).then_inc(xres_loaded.sem, 16)

        def finish(b, r, u):
            load_residual(b, r, u)
            wait(sp, ot_done, u, 1)
            sp.dma_start(out_tok[b, bass.ds(r * M, M), :].rearrange("(q p) c -> p q c", p=P), ot[:]
                         ).then_inc(out_stored.sem, 16)

        def period(b, r, u, par, finishes, prepares, bottom=False):
            if prepares:
                prep(b, r + 1, u + 1, 1 - par, bottom=bottom)
            if finishes:
                finish(b, r - 1, u - 1)

        batch(sp, prep, period, finish)
        wait(sp, out_stored, B * NR - 1, 16)

    @block.scalar
    def _(act):
        def norm(b, u, par):
            scale, bias = g2_now[:, 0:1], g2_now[:, 1:2]

            def put(dst, columns):
                return nc.scalar.activation(dst, columns, ACT.Identity, bias=bias, scale=scale)

            wait(act, xh_loaded, u, 32)
            wait(act, conv_mm, u - 1, 2 * KC)
            wait(act, sums_done, u - 1, 2)
            wait(act, sob, u - 1, 1)
            put(sn[:, :, :, 1:W + 1].rearrange("p k r w -> p (k r) w"), xh[:].rearrange("p k r w -> p (k r) w"))
            put(sn[:, :, :, 0], xh[:, :, :, 1])
            put(sn[:, :, :, W + 1], xh[:, :, :, W - 2]).then_inc(sn_done.sem, 1)
            inner = xh[:, :, 1:ROWS + 1, :]
            put(hs[:, par, :, :, 1:W + 1], inner)
            put(hs[:, par, :, :, 0], inner[:, :, :, W - 1])
            put(hs[:, par, :, :, W + 1], inner[:, :, :, 0]).then_inc(hs_done.sem, 1)

        def squares(u):
            wait(act, sob, u, 4)
            nc.scalar.activation(flat(gy[:]), flat(gy[:]), ACT.Square, scale=0.5)
            nc.scalar.activation(flat(gx[:]), flat(gx[:]), ACT.Square, scale=0.5).then_inc(squared.sem, 1)
            wait(act, squared, u, 1)
            nc.scalar.activation(flat(gy[:]), flat(gy[:]), ACT.Identity, bias=one[:])
            nc.scalar.activation(flat(gx[:]), flat(gx[:]), ACT.Identity, bias=one[:]).then_inc(squared.sem, 1)

        def first_reciprocal(u):
            wait(act, coef, u, 3)
            nc.scalar.activation(flat(rec[:]), flat(den[:]), ACT.Ln).then_inc(den_log.sem, 1)
            wait(act, den_log, u, 1)
            nc.scalar.activation(flat(rec[:]), flat(rec[:]), ACT.Exp, scale=-1.0).then_inc(rec_done.sem, 1)

        def fluxes(u, conv):
            if conv == 0:
                wait(act, e2_done, u - 1, 1)
                wait(act, da_done, u - 1, 1)
            else:
                wait(act, dv_done, u - 1, 1)
                wait(act, ay_used, u - 1, 1)
            for k in range(KC):
                scale, bias = bn_s[:, conv, k:k + 1], bn_b[:, conv, k:k + 1]
                ps = conv_ps[:, conv * KC + k]
                wait(act, conv_mm, u, conv * KC + k + 1)
                if conv == 0:
                    nc.scalar.activation(ax[:, k, :, 1:W + 1], ps, ACT.Relu, bias=bias, scale=scale)
                    nc.scalar.activation(ax[:, k, :, 0], ps[:, :, W - 1], ACT.Relu, bias=bias, scale=scale)
                    last = nc.scalar.activation(ax[:, k, :, W + 1], ps[:, :, 0], ACT.Relu, bias=bias, scale=scale)
                else:
                    last = nc.scalar.activation(ay[:, k], ps, ACT.Relu, bias=bias, scale=scale)
            last.then_inc((ay_done if conv else ax_done).sem, 1)

        def finish_relu(u):
            wait(act, h_done, u, K_STEPS)
            wait(act, fo_T, u - 1, 1)
            for k in range(KC):
                last = nc.scalar.activation(fo[:, k], hb[:, (K_STEPS - 1) % 3, k, :, 1:W + 1], ACT.Relu,
                                            bias=bn_b[:, 2, k:k + 1], scale=bn_s[:, 2, k:k + 1])
            last.then_inc(fo_done.sem, 1)

        def finish_out(u):
            wait(act, fo_T, u, 1)
            wait(act, out_stored, u - 1, 16)
            for k in range(KC):
                last = nc.scalar.copy(ot[:, :, bass.ds(k, P, KC)], conv_ps[:, KC + k])
            last.then_inc(ot_done.sem, 1)

        def prep(b, r, u, par, top=False, bottom=False):
            nc.scalar.copy(g2_now[:, 0:1], g2_scale[:, bass.ds(b, 1)])
            nc.scalar.copy(g2_now[:, 1:2], g2_shift[:, bass.ds(b, 1)]).then_inc(batch_norm, 1)
            act.wait_ge(batch_norm, b + 1)
            norm(b, u, par)
            squares(u)
            fluxes(u, 0)
            first_reciprocal(u)
            fluxes(u, 1)

        def finish(b, r, u):
            finish_relu(u)
            finish_out(u)

        def period(b, r, u, par, finishes, prepares, bottom=False):
            if finishes:
                finish_relu(u - 1)
            if prepares:
                norm(b, u + 1, 1 - par)
            if finishes:
                finish_out(u - 1)
            if prepares:
                squares(u + 1)
                fluxes(u + 1, 0)
                first_reciprocal(u + 1)
                fluxes(u + 1, 1)

        batch(act, prep, period, finish)

    @block.gpsimd
    def _(pool):
        tt = nc.gpsimd.tensor_tensor

        def sums(u):
            wait(pool, sn_done, u, 1)
            wait(pool, sob, u - 1, 4)
            rows = "p k r w -> p (k r) w"
            left, right = sn[:, :, :, 0:W].rearrange(rows), sn[:, :, :, 2:W + 2].rearrange(rows)
            tt(sum_w[:].rearrange(rows), left, right, ALU.add).then_inc(sums_done.sem, 1)
            tt(dif_w[:].rearrange(rows), right, left, ALU.subtract).then_inc(sums_done.sem, 1)

        def old_factor(u, par):
            wait(pool, coef, u, 8)
            tt(flat(c_old[:, par]), flat(dd[:]), flat(dbx[:]), ALU.subtract).then_inc(old_done.sem, 1)
            wait(pool, old_done, u, 1)
            tt(flat(c_old[:, par]), flat(c_old[:, par]), flat(dby[:]), ALU.subtract).then_inc(old_done.sem, 1)

        def channel_factors(u, par):
            wait(pool, ay_done, u, 1)
            dv = src2
            wait(pool, coef, u, 8)
            wait(pool, acc_done, u - 1, 2)
            tt(flat(dv[:]), flat(dd[:]), flat(ay[:]), ALU.mult).then_inc(dv_done.sem, 1)
            wait(pool, dv_done, u, 1)
            tt(c_moved[:, par, 0], dby[:, 0], dv[:, 0], ALU.subtract)
            tt(c_moved[:, par, 1], dby[:, 1], dv[:, 1], ALU.add)
            tt(c_same[:, par, 0], dby[:, 0], dv[:, 0], ALU.add)
            tt(c_same[:, par, 1], dby[:, 1], dv[:, 1], ALU.subtract).then_inc(dv_done.sem, 1)

        def second_source(u, par):
            wait(pool, src_done, u, 1)
            wait(pool, old_done, u, 2)
            wait(pool, dv_done, u, 2)
            tt(src2[:], c_old[:, par], hs[:, par, :, :, 1:W + 1], ALU.mult).then_inc(src_steps.sem, 1)
            wait(pool, src_steps, u, 1)
            tt(flat(src2[:]), flat(src2[:]), flat(src[:, par]), ALU.add).then_inc(src_steps.sem, 1)

        def first_source(u, par):
            wait(pool, e2_done, u, 4)
            wait(pool, acc_done, u - 1, 1)
            tt(src1[:], c_own[:, par], hs[:, par, :, :, 1:W + 1], ALU.mult).then_inc(src_steps.sem, 1)
            wait(pool, src_steps, u, 3)
            tt(flat(src1[:]), flat(src1[:]), flat(src2[:]), ALU.add).then_inc(src_steps.sem, 1)

        def own_term(u, par, it):
            wait(pool, h_done, u, it)
            if it == 1:
                wait(pool, acc_done, u - 1, K_STEPS)
            else:
                wait(pool, acc_done, u, it)
            tt(q_own[:], c_own[:, par], state(par, it)[:, :, :, 1:W + 1], ALU.mult).then_inc(q_own_done.sem, 1)
            if it in POOL_SUMS:
                wait(pool, q_own_done, u, it)
                if it == 1:
                    wait(pool, src_steps, u, 2)
                    old = src2
                else:
                    wait(pool, q_old_done, u, 2 * (it - 2) + 2)
                    old = q_old
                tt(flat(q_own[:]), flat(q_own[:]), flat(old[:]), ALU.add).then_inc(q_pool_done.sem, 1)

        def old_term(u, par, it):
            wait(pool, h_done, u, it - 1)
            if it > 2 and it - 1 in POOL_SUMS:
                wait(pool, q_pool_done, u, POOL_SUMS.index(it - 1) + 1)
            elif it > 2:
                wait(pool, acc_done, u, it)
            tt(q_old[:], c_old[:, par], state(par, it - 1)[:, :, :, 1:W + 1], ALU.mult).then_inc(q_old_done.sem, 1)
            wait(pool, q_old_done, u, 2 * (it - 2) + 1)
            tt(flat(q_old[:]), flat(q_old[:]), flat(src[:, par]), ALU.add).then_inc(q_old_done.sem, 1)

        def add_residual(u):
            wait(pool, fo_done, u, 1)
            wait(pool, xres_loaded, u, 16)
            tt(flat(fo[:]), flat(fo[:]), flat(xres[:]), ALU.add).then_inc(added.sem, 1)

        def prep(b, r, u, par, top=False, bottom=False):
            sums(u)
            old_factor(u, par)
            channel_factors(u, par)
            second_source(u, par)
            first_source(u, par)

        def finish(b, r, u):
            add_residual(u)

        def period(b, r, u, par, finishes, prepares, bottom=False):
            if prepares:
                sums(u + 1)
            own_term(u, par, 1)
            old_term(u, par, 2)
            if finishes:
                add_residual(u - 1)
            own_term(u, par, 2)
            old_term(u, par, 3)
            own_term(u, par, 3)
            old_term(u, par, 4)
            if prepares:
                old_factor(u + 1, 1 - par)
            own_term(u, par, 4)
            if prepares:
                channel_factors(u + 1, 1 - par)
                second_source(u + 1, 1 - par)
                first_source(u + 1, 1 - par)

        batch(pool, prep, period, finish)

    @block.vector
    def _(dve):
        tt, stt, ts = nc.vector.tensor_tensor, nc.vector.scalar_tensor_tensor, nc.vector.tensor_scalar

        def step(u, par, it, between=None):
            h = state(par, it)
            if it == 0:
                wait(dve, hs_done, u, 1)
                wait(dve, da_done, u, 3)
                wait(dve, dv_done, u, 2)
            else:
                wait(dve, wrapped, u, it)
                wait(dve, h_done, u, it)
            tt(q_left[:], c_left[:, par], h[:, :, :, 0:W], ALU.mult).then_inc(q_left_done.sem, 1)
            tt(q_right[:], c_right[:, par], h[:, :, :, 2:W + 2], ALU.mult).then_inc(q_right_done.sem, 1)
            if it in SIDE_SUMS:
                wait(dve, q_right_done, u, it + 1)
                wait(dve, q_left_done, u, it + 1)
                tt(flat(q_left[:]), flat(q_left[:]), flat(q_right[:]), ALU.add).then_inc(q_sides_done.sem, 1)
            for k in range(KC):
                last = tt(q_same[:, k], c_same[:, par, k], h[:, 1 - k, :, 1:W + 1], ALU.mult)
            last.then_inc(q_same_done.sem, 1)
            wait(dve, moved, u, it + 1)
            tt(flat(q_moved[:]), flat(c_moved[:, par]), flat(moved_ps[:]), ALU.mult).then_inc(q_moved_done.sem, 1)
            wait(dve, q_moved_done, u, 2 * it + 1)
            wait(dve, q_same_done, u, it + 1)
            tt(flat(q_moved[:]), flat(q_moved[:]), flat(q_same[:]), ALU.add).then_inc(q_moved_done.sem, 1)
            if between:
                between()
            wait(dve, q_moved_done, u, 2 * it + 2)
            wait(dve, acc_done, u, it + 1)
            if it == 1:
                wait(dve, fo_done, u - 1, 1)
            if it == 3:
                wait(dve, q_old_done, u, 2)
            if it == 4:
                wait(dve, q_old_done, u, 4)
            new = hb[:, it % 3]
            tt(new[:, :, :, 1:W + 1], acc_ps[:], q_moved[:], ALU.add).then_inc(h_done.sem, 1)
            wait(dve, h_done, u, it + 1)
            if it < K_STEPS - 1:
                nc.vector.tensor_copy(new[:, :, :, 0], new[:, :, :, W])
                nc.vector.tensor_copy(new[:, :, :, W + 1], new[:, :, :, 1]).then_inc(wrapped.sem, 1)
            else:
                nc.vector.tensor_copy(new[:, :, :, W + 1], new[:, :, :, 1]).then_inc(wrapped.sem, 1)

        def sobel(u):
            wait(dve, sums_done, u, 2)
            wait(dve, sn_done, u, 1)
            wait(dve, coef, u - 1, 8)
            rows = "p k r w -> p (k r) w"
            stt(sum_w[:].rearrange(rows), sn[:, :, :, 1:W + 1].rearrange(rows), 2.0, sum_w[:].rearrange(rows),
                ALU.mult, ALU.add).then_inc(sob.sem, 1)
            tt(flat(gx[:]), flat(dif_w[:, :, 0:ROWS]), flat(dif_w[:, :, 2:ROWS + 2]), ALU.add).then_inc(sob.sem, 1)
            wait(dve, sob, u, 1)
            tt(flat(gy[:]), flat(sum_w[:, :, 2:ROWS + 2]), flat(sum_w[:, :, 0:ROWS]), ALU.subtract).then_inc(sob.sem, 1)
            wait(dve, sob, u, 2)
            stt(flat(gx[:]), flat(dif_w[:, :, 1:ROWS + 1]), 2.0, flat(gx[:]), ALU.mult, ALU.add).then_inc(sob.sem, 1)

        def denominator(u):
            wait(dve, squared, u, 2)
            tt(flat(pq[:]), flat(gy[:]), flat(gx[:]), ALU.mult).then_inc(coef.sem, 1)
            tt(flat(den[:]), flat(gy[:]), flat(gx[:]), ALU.add).then_inc(coef.sem, 1)
            wait(dve, coef, u, 2)
            stt(flat(den[:]), flat(den[:]), 2 * DT, flat(pq[:]), ALU.mult, ALU.add).then_inc(coef.sem, 1)

        def diffusivities(u):
            wait(dve, rec_done, u, 1)
            tt(flat(den[:]), flat(den[:]), flat(rec[:]), ALU.mult).then_inc(coef.sem, 1)
            wait(dve, coef, u, 4)
            stt(flat(rec[:]), flat(den[:]), 2.0, flat(rec[:]), ALU.subtract, ALU.mult).then_inc(coef.sem, 1)
            wait(dve, coef, u, 5)
            wait(dve, dv_done, u - 1, 2)
            wait(dve, old_done, u - 1, 2)
            stt(flat(dd[:]), flat(pq[:]), -1.0, flat(rec[:]), ALU.mult, ALU.mult).then_inc(coef.sem, 1)
            stt(flat(dbx[:]), flat(gx[:]), -2 * DT, flat(rec[:]), ALU.mult, ALU.mult).then_inc(coef.sem, 1)
            stt(flat(dby[:]), flat(gy[:]), -2 * DT, flat(rec[:]), ALU.mult, ALU.mult).then_inc(coef.sem, 1)

        def row_factors(u, par):
            wait(dve, coef, u, 8)
            wait(dve, ax_done, u, 1)
            da = c_own[:, par]
            tt(da, dd[:], ax[:, :, :, 1:W + 1], ALU.mult).then_inc(da_done.sem, 1)
            wait(dve, da_done, u, 1)
            tt(flat(c_left[:, par]), flat(dbx[:]), flat(da), ALU.subtract).then_inc(da_done.sem, 1)
            tt(flat(c_right[:, par]), flat(dbx[:]), flat(da), ALU.add).then_inc(da_done.sem, 1)

        def own_factor_w(u, par):
            wait(dve, coef, u, 8)
            e2 = den
            wait(dve, ax_done, u, 1)
            tt(e2[:], ax[:, :, :, 0:W], ax[:, :, :, 2:W + 2], ALU.subtract).then_inc(e2_done.sem, 1)
            stt(src[:, par], dd[:], 2 * DT, hs[:, par, :, :, 1:W + 1], ALU.mult, ALU.mult).then_inc(src_done.sem, 1)

        def own_factor(u, par):
            e2, e2y = den, pq
            wait(dve, ay_moved, u, 1)
            wait(dve, ay_done, u, 1)
            tt(e2y[:, 0], conv_ps[:, 0], ay[:, 1], ALU.subtract)
            tt(e2y[:, 1], ay[:, 0], conv_ps[:, 1], ALU.subtract).then_inc(ay_used.sem, 1)
            wait(dve, ay_used, u, 1)
            wait(dve, e2_done, u, 1)
            tt(flat(e2[:]), flat(e2[:]), flat(e2y[:]), ALU.add).then_inc(e2_done.sem, 1)
            wait(dve, e2_done, u, 2)
            wait(dve, da_done, u, 3)
            stt(flat(c_own[:, par]), flat(dd[:]), -1.0, flat(e2[:]), ALU.mult, ALU.mult).then_inc(e2_done.sem, 2)

        def prep(b, r, u, par, top=False, bottom=False):
            sobel(u)
            denominator(u)
            diffusivities(u)
            row_factors(u, par)
            own_factor_w(u, par)
            own_factor(u, par)

        def finish(b, r, u):
            pass

        def period(b, r, u, par, finishes, prepares, bottom=False):
            def last_factors():
                row_factors(u + 1, 1 - par)
                own_factor_w(u + 1, 1 - par)
                own_factor(u + 1, 1 - par)

            step(u, par, 0)
            step(u, par, 1, (lambda: sobel(u + 1)) if prepares else None)
            step(u, par, 2, (lambda: denominator(u + 1)) if prepares else None)
            step(u, par, 3, (lambda: diffusivities(u + 1)) if prepares else None)
            step(u, par, 4, last_factors if prepares else None)

        batch(dve, prep, period, finish)

    @block.tensor
    def _(pe):
        def step(u, par, it, between=None):
            h = state(par, it)
            if it == 0:
                wait(pe, hs_done, u, 1)
                wait(pe, h_done, u - 1, K_STEPS)
            else:
                wait(pe, h_done, u, it)
            nc.tensor.matmul(moved_ps[:, 0], down_one[:], h[:, 1, :, 1:W + 1], start=True, stop=True)
            nc.tensor.matmul(moved_ps[:, 1], up_one[:], h[:, 0, :, 1:W + 1], start=True, stop=True
                             ).then_inc(moved.sem, 1)
            if between:
                between()
            if it in SIDE_SUMS:
                terms = [(q_left, q_sides_done, SIDE_SUMS.index(it) + 1)]
            else:
                terms = [(q_left, q_left_done, it + 1), (q_right, q_right_done, it + 1)]
            if it == 0:
                terms.append((src1, src_steps, 4))
            elif it in POOL_SUMS:
                terms.append((q_own, q_pool_done, POOL_SUMS.index(it) + 1))
            else:
                terms.insert(0, (src2, src_steps, 2) if it == 1 else (q_old, q_old_done, 2 * (it - 2) + 2))
                terms.append((q_own, q_own_done, it))
            for i, (term, ready, count) in enumerate(terms):
                wait(pe, ready, u, count)
                for k in range(KC):
                    last = nc.tensor.matmul(acc_ps[:, k], ident[:], term[:, k], start=(i == 0), stop=(i == len(terms) - 1))
            last.then_inc(acc_done.sem, 1)

        def convolve(u, first, end, top, bottom):
            last_full = 0 if bottom else 2
            order = [(1, 1)] + [(i, j) for i in range(3) for j in range(3)
                                if (i, j) not in ((1, 1), (last_full, 1))] + [(last_full, 1)]
            for at in range(first, end):
                conv, k, n = at // (9 * KC), at // 9 % KC, at % 9
                if at == 0:
                    wait(pe, sn_done, u, 1)
                    wait(pe, ay_used, u - 1, 1)
                if at == 9 * KC:
                    wait(pe, ot_done, u - 2, 1)
                i, j = order[n]
                r0 = 1 if top and i == 0 else 0
                r1 = ROWS - 1 if bottom and i == 2 else ROWS
                w0, w1 = max(0, 1 - j), min(W, W + 1 - j)
                mm = nc.tensor.matmul(conv_ps[:, conv * KC + k, r0:r1, w0:w1], taps[:, conv, k, 3 * i + j, :],
                                      sn[:, k, r0 + i:r1 + i, w0 + j:w1 + j],
                                      start=(n == 0), stop=(n == 8), skip_group_check=(0 < n < 8))
                if n == 8:
                    mm.then_inc(conv_mm.sem, 1)

        def move_ay(u):
            wait(pe, ay_done, u, 1)
            wait(pe, ax_done, u, 1)
            nc.tensor.matmul(conv_ps[:, 0], down_one[:], ay[:, 1], start=True, stop=True)
            nc.tensor.matmul(conv_ps[:, 1], up_one[:], ay[:, 0], start=True, stop=True).then_inc(ay_moved.sem, 1)

        def finish_T(u, after_prep):
            wait(pe, added, u, 1)
            wait(pe, ay_done, u + after_prep, 1)
            for k in range(KC):
                for r in range(ROWS):
                    last = nc.tensor.transpose(conv_ps[:, KC + k, r, :], fo[:, k, r, :], ident[:])
            last.then_inc(fo_T.sem, 1)

        def prep(b, r, u, par, top=False, bottom=False):
            wait(pe, ot_done, u - 1, 1)
            convolve(u, 0, 2 * KC * 9, top, bottom)
            move_ay(u)

        def finish(b, r, u):
            finish_T(u, 0)

        def period(b, r, u, par, finishes, prepares, bottom=False):
            step(u, par, 0)
            for it in range(1, K_STEPS):
                if prepares:
                    convolve(u + 1, CONV_PIECES[it - 1], CONV_PIECES[it], False, bottom)
                if it == 2 and finishes:
                    finish_T(u - 1, 1)
                step(u, par, it, (lambda: move_ay(u + 1)) if it == 4 and prepares else None)

        batch(pe, prep, period, finish)


def constants():
    N = 16
    ident = np.eye(P, dtype=np.float32)
    avg_all = np.full((P, P), 1.0 / P, np.float32)
    select = np.zeros((6 * N, 2 * N, P), np.uint16)
    for part in range(3):
        for n in range(2 * N):
            select[2 * N * part + n, n, :] = 0x3F80
    avg4 = np.kron(np.eye(P // 4, dtype=np.float32), np.full((4, 4), 0.25, np.float32))
    down_one = np.roll(ident, 1, axis=1)
    up_one = np.roll(ident, -1, axis=1)
    return {"avg4": avg4, "down_one": down_one, "up_one": up_one, "ident": ident, "avg_all": avg_all, "select": select}


def arrays_of(inputs):
    L0 = {k[len("L0_conv_"):]: np.asarray(v) for k, v in inputs.items() if k.startswith("L0_conv_")}
    r = {"x": np.asarray(inputs["x"])}
    for k in ("in_proj_w", "x_proj_w", "dt_proj_w", "out_proj_w", "proj_w"):
        r[k + "T"] = np.ascontiguousarray(L0.pop(k).T)
    for k in ("conv_b", "dt_proj_b", "D", "ln_g", "ln_b"):
        L0[k] = L0[k].reshape(-1, P).T
    L0["proj_b"] = L0["proj_b"].reshape(P, -1)
    r.update(L0)
    L1 = {k[len("L1_conv_"):]: np.asarray(v) for k, v in inputs.items() if k.startswith("L1_conv_")}
    r["taps_w"] = np.stack([L1[k].reshape(9, P, 2).transpose(1, 0, 2) for k in ("wg", "wg1")], axis=1)
    r["bn_in"] = np.stack([np.stack([L1[f"{g}_{v}"].reshape(P, 2) for v in ("gamma", "beta", "mean", "var")], axis=1)
                           for g in ("g", "g1", "out")], axis=1)
    r.update(constants())
    return {k: np.ascontiguousarray(v) for k, v in r.items()}


def kernel(**inputs):
    import concourse.bacc as bacc
    from concourse.bass_utils import run_bass_kernel_spmd

    nc = bacc.Bacc("TRN2", target_bir_lowering=False, num_devices=1)
    given = arrays_of(inputs)
    arrays = {f"in_{k}": v for k, v in given.items()}
    a = {k: nc.dram_tensor(f"in_{k}", list(v.shape), mybir.dt.from_np(v.dtype), kind="ExternalInput").ap()
         for k, v in given.items()}
    B, H, W, C = given["x"].shape
    a["x1_dram"] = nc.dram_tensor("x1_dram", [B, C // P, P, H * W], F32, kind="Internal").ap()
    a["out"] = nc.dram_tensor("out_0", [B, H, W, C], F32, kind="ExternalOutput").ap()
    token_mixer(nc, a)
    return run_bass_kernel_spmd(nc, [arrays], core_ids=[0]).results[0]["out_0"]
```
